# Optimizing a Trainium2 kernel written in Bass

```python
import numpy as np
import jax
import jax.numpy as jnp

def _softmax(x, axis=-1):
    return jax.nn.softmax(x, axis=axis)

def _gelu(x):
    return jax.nn.gelu(x, approximate=True)

def _silu(x):
    return jax.nn.silu(x)

def _sigmoid(x):
    return jax.nn.sigmoid(x)

def _layernorm(x, axis=-1, eps=1e-05):
    m = jnp.mean(x, axis=axis, keepdims=True)
    v = jnp.var(x, axis=axis, keepdims=True)
    return (x - m) / jnp.sqrt(v + eps)

def _scatter_add(tgt, idx, src, axis=0):
    return tgt.at[idx].add(src)

def _segment_sum(src, seg, n):
    return jax.ops.segment_sum(src, seg, n)
kernel_name = 'mk_lm_tower_d1_tok_ids4096_r4_edfbcd'

def setup_inputs(seed: int=0):
    np.random.seed(seed)
    _w = jnp.asarray

    def _rec_inputs():
        import jax
        import jax.numpy as jnp
        _rk = jax.random.key(seed)
        x = jax.random.randint(jax.random.fold_in(_rk, 1), (64, 128), 0, 31993, jnp.int32)
        return x
    x = _rec_inputs()

    def _L0_tok_setup():
        import jax, jax.numpy as jnp
        import numpy as np
        VOCAB = 8000
        DIM = 1024
        RANK = 16
        BATCH, SEQ = (4, 512)
        key = jax.random.key(seed)
        k1, k2, k3 = jax.random.split(key, 3)
        input_ids = jax.random.randint(k1, (BATCH, SEQ), 0, VOCAB)
        lora_down = jax.random.normal(k2, (VOCAB, RANK), dtype=jnp.float32)
        lora_up = jax.random.normal(k3, (RANK, DIM), dtype=jnp.float32)
        return {'input_ids': input_ids, 'lora_down': lora_down, 'lora_up': lora_up}
    _L0_tok_all = _L0_tok_setup()
    _L0_tok_in = {k: v for k, v in _L0_tok_all.items() if k in ('lora_down', 'lora_up')}
    del _L0_tok_all

    def _L0_attn_setup():
        import jax, jax.numpy as jnp
        import numpy as np
        import math
        D_MODEL = 512
        D_STATE = 16
        EXPAND = 2
        D_INNER = D_MODEL * EXPAND
        DT_RANK = math.ceil(D_MODEL / 16)
        BATCH, SEQ_LEN = (2, 128)
        key = jax.random.key(seed)
        ks = jax.random.split(key, 6)
        x = jax.random.normal(ks[0], (BATCH, SEQ_LEN, D_INNER), dtype=jnp.float32)
        A_log = jnp.log(jax.random.uniform(ks[1], (D_INNER, D_STATE), minval=0.5, maxval=16.0, dtype=jnp.float32))
        D = jnp.ones((D_INNER,), dtype=jnp.float32)
        x_proj_w = 0.02 * jax.random.normal(ks[2], (DT_RANK + 2 * D_STATE, D_INNER), dtype=jnp.float32)
        dt_init_std = DT_RANK ** (-0.5)
        dt_proj_w = jax.random.uniform(ks[3], (D_INNER, DT_RANK), minval=-dt_init_std, maxval=dt_init_std, dtype=jnp.float32)
        dt = jnp.exp(jax.random.uniform(ks[4], (D_INNER,), dtype=jnp.float32) * (math.log(0.1) - math.log(0.001)) + math.log(0.001))
        dt = jnp.clip(dt, 0.0001, None)
        dt_proj_b = dt + jnp.log(-jnp.expm1(-dt))
        return {'x': x, 'A_log': A_log, 'D': D, 'x_proj_w': x_proj_w, 'dt_proj_w': dt_proj_w, 'dt_proj_b': dt_proj_b}
    _L0_attn_all = _L0_attn_setup()
    _L0_attn_in = {k: v for k, v in _L0_attn_all.items() if k in ('A_log', 'D', 'x_proj_w', 'dt_proj_w', 'dt_proj_b')}
    del _L0_attn_all

    def _L0_ffn_setup():
        import jax, jax.numpy as jnp
        import numpy as np
        FP8_MAX = 448.0

        def quantize_tensorwise(x):
            amax = jnp.max(jnp.abs(x))
            inv_scale = jnp.maximum(amax, jnp.asarray(1e-12, x.dtype)) / FP8_MAX
            q = (x / inv_scale).astype(jnp.float8_e4m3fn)
            return (q, inv_scale)
        key = jax.random.key(seed)
        k1, k2, k3 = jax.random.split(key, 3)
        x = jax.random.normal(k1, (4, 256, 1024), dtype=jnp.float32)
        weight = jax.random.normal(k2, (1024, 1024), dtype=jnp.float32) * 0.02
        bias = jax.random.normal(k3, (1024,), dtype=jnp.float32)
        return {'x': x, 'weight': weight, 'bias': bias}
    _L0_ffn_all = _L0_ffn_setup()
    _L0_ffn_in = {k: v for k, v in _L0_ffn_all.items() if k in ('weight', 'bias')}
    del _L0_ffn_all
    return {'x': x, 'L0_tok_lora_down': _L0_tok_in['lora_down'], 'L0_tok_lora_up': _L0_tok_in['lora_up'], 'L0_attn_A_log': _L0_attn_in['A_log'], 'L0_attn_D': _L0_attn_in['D'], 'L0_attn_x_proj_w': _L0_attn_in['x_proj_w'], 'L0_attn_dt_proj_w': _L0_attn_in['dt_proj_w'], 'L0_attn_dt_proj_b': _L0_attn_in['dt_proj_b'], 'L0_ffn_weight': _L0_ffn_in['weight'], 'L0_ffn_bias': _L0_ffn_in['bias']}

def reference(x, L0_tok_lora_down, L0_tok_lora_up, L0_attn_A_log, L0_attn_D, L0_attn_x_proj_w, L0_attn_dt_proj_w, L0_attn_dt_proj_b, L0_ffn_weight, L0_ffn_bias):
    import jax
    import jax.numpy as jnp

    def _L0_tok_ref(input_ids, lora_down, lora_up):
        import jax, jax.numpy as jnp
        import numpy as np
        VOCAB = 8000
        DIM = 1024
        RANK = 16
        BATCH, SEQ = (4, 512)
        down_rows = lora_down[input_ids]
        return jnp.einsum('bsr,rd->bsd', down_rows, lora_up)

    def _L0_attn_ref(x, A_log, D, x_proj_w, dt_proj_w, dt_proj_b):
        import jax, jax.numpy as jnp
        import numpy as np
        import math
        D_MODEL = 512
        D_STATE = 16
        EXPAND = 2
        D_INNER = D_MODEL * EXPAND
        DT_RANK = math.ceil(D_MODEL / 16)
        BATCH, SEQ_LEN = (2, 128)
        A = -jnp.exp(A_log)
        xp = jnp.einsum('bld,rd->blr', x, x_proj_w)
        dt_in = xp[..., :DT_RANK]
        B = xp[..., DT_RANK:DT_RANK + D_STATE]
        C = xp[..., DT_RANK + D_STATE:]
        dt = jax.nn.softplus(jnp.einsum('blr,dr->bld', dt_in, dt_proj_w) + dt_proj_b)
        dA = jnp.exp(dt[..., None] * A)
        dBx = dt[..., None] * B[:, :, None, :] * x[..., None]

        def step(h, inp):
            dA_t, dBx_t, C_t = inp
            h = dA_t * h + dBx_t
            y = jnp.einsum('bdn,bn->bd', h, C_t)
            return (h, y)
        h0 = jnp.zeros((x.shape[0], D_INNER, D_STATE), dtype=x.dtype)
        _, ys = jax.lax.scan(step, h0, (jnp.moveaxis(dA, 1, 0), jnp.moveaxis(dBx, 1, 0), jnp.moveaxis(C, 1, 0)))
        y = jnp.moveaxis(ys, 0, 1) + D * x
        return y

    def _L0_ffn_ref(x, weight, bias):
        import jax, jax.numpy as jnp
        import numpy as np
        FP8_MAX = 448.0

        def quantize_tensorwise(x):
            amax = jnp.max(jnp.abs(x))
            inv_scale = jnp.maximum(amax, jnp.asarray(1e-12, x.dtype)) / FP8_MAX
            q = (x / inv_scale).astype(jnp.float8_e4m3fn)
            return (q, inv_scale)
        out_shape = (*x.shape[:-1], weight.shape[0])
        xm = x.reshape(-1, x.shape[-1])
        fp8_x, x_inv_scale = quantize_tensorwise(xm)
        fp8_wt, w_inv_scale = quantize_tensorwise(weight.T)
        acc = jnp.matmul(fp8_x.astype(jnp.float32), fp8_wt.astype(jnp.float32))
        out = acc * (x_inv_scale * w_inv_scale) + bias.astype(jnp.float32)
        return out.reshape(out_shape).astype(x.dtype)
    h = _L0_tok_ref(x, L0_tok_lora_down, L0_tok_lora_up)
    h = h + _L0_attn_ref(_layernorm(h, axis=-1), L0_attn_A_log, L0_attn_D, L0_attn_x_proj_w, L0_attn_dt_proj_w, L0_attn_dt_proj_b)
    h = h + _L0_ffn_ref(_layernorm(h, axis=-1), L0_ffn_weight, L0_ffn_bias)
    return h

_drawn_inputs = setup_inputs


def setup_inputs(seed=0):
    import zlib

    import numpy as np

    out = dict(_drawn_inputs(seed))
    spreads = {'L0_attn_D': (1.0, 0.2)}
    factors = {}
    for name, (base, spread) in spreads.items():
        noise = np.random.default_rng([zlib.crc32(name.encode()), seed]).standard_normal(out[name].shape)
        drawn = base * np.exp(spread * noise) if base else spread * noise
        out[name] = jnp.asarray(drawn.astype(out[name].dtype))
    for name, factor in factors.items():
        out[name] = (out[name] * factor).astype(out[name].dtype)
    return out
```

```python
import concourse.bass as bass
from concourse import mybir
from contextlib import ExitStack

FP32 = mybir.dt.float32
BF16 = mybir.dt.bfloat16
I32 = mybir.dt.int32
U32 = mybir.dt.uint32
ALU = mybir.AluOpType
ACT = mybir.ActivationFunctionType
AX = mybir.AxisListType

P = 128
BATCH, SEQ = 64, 128
VOCAB, RANK = 8000, 16
DIM = 1024
STATE = 16
DTR = 32
XP = DTR + 2 * STATE
KT = DIM // P
GB = 4
GROUPS = BATCH // GB
GT = GB * SEQ
HT = KT // 2
HD = HT * P
U0 = 32
UNITS = STATE * 2
EPS = 1e-5
FP8_MAX = 448.0
EXP_BITS = 0x7F800000
MIN_NORMAL = 2.0 ** -6
ROUND = 1.5 * 2.0 ** 20

LAG = 3
NDA, NH, NP = 2, 2, 4
DX_AT = {4: 0, 5: 1}
F_AT = 6
PREP_AT = {
    0: {10: [("Z", 0)], 16: [("U", 0), ("Z", 1)], 22: [("U", 1)]},
    1: {8: [("E", 0)], 9: [("E", 1)], 10: [("X", 0)], 11: [("X", 1)], 12: [("X", 2)], 13: [("X", 3)],
        14: [("P", 0)], 15: [("Z", 0)], 16: [("B", 0)], 21: [("U", 0), ("Z", 1)], 27: [("U", 1)]},
}
PROLOGUE = [("E", 0), ("E", 1), ("X", 0), ("X", 1), ("X", 2), ("X", 3), ("P", 0), ("B", 0),
            ("Z", 0), ("U", 0), ("Z", 1), ("U", 1)]
Z_AT = {h: {q: u for u, jobs in PREP_AT[h].items() for kind, q in jobs if kind == "Z"} for h in (0, 1)}
ACT_AFTER, DT_AFTER = 3, 4


def slot_plan(h, final, prep):
    plan = []
    for u in range(UNITS):
        plan.append(("S", u))
        if final and u == F_AT:
            plan += [("F", 0), ("F", 1)]
        if prep:
            plan += PREP_AT[h].get(u, [])
    return plan


PLAN_FIRST = slot_plan(0, False, True)
PLAN = [slot_plan(0, True, True), slot_plan(1, True, True)]
PLAN_LAST = slot_plan(1, True, False)
N0 = len(PROLOGUE)
NG = len(PLAN[0]) + len(PLAN[1])
assert N0 % 2 == 0 and NG % 2 == 0 and UNITS % NP == 0 and UNITS % NH == 0 and UNITS % NDA == 0


def static(g, value):
    return isinstance(g, int) and g == value


def slot_at(g, h, kind, arg):
    if static(g, 0) and h == 0:
        return 2 + PLAN_FIRST.index((kind, arg))
    if static(g, GROUPS - 1) and h == 1:
        return len(PLAN[0]) + PLAN_LAST.index((kind, arg))
    return (len(PLAN[0]) if h else 0) + PLAN[h].index((kind, arg))


def slot_no(g, h, kind, arg):
    return g * NG + (N0 - 2 + slot_at(g, h, kind, arg))


def slot_side(g, h, kind, arg):
    return slot_at(g, h, kind, arg) % 2


TAIL = slot_no(GROUPS - 1, 1, "S", UNITS - 1) + 1


def setup_stage(nc, d, s):
    with ExitStack() as ctx:
        sb = lambda name, shape, dt: ctx.enter_context(nc.sbuf_tensor(name, shape, dt))
        pb = lambda name, shape, dt: ctx.enter_context(nc.psum_tensor(name, shape, dt))
        sem = lambda name: ctx.enter_context(nc.semaphore(name))
        ids = sb("ids", [P, BATCH], I32)
        idf = sb("idf", [P, 3, BATCH], FP32)
        idx = sb("idx", [P, BATCH], U32)
        araw = sb("araw", [P, KT, STATE], FP32)
        dvec = sb("dvec", [P, KT], FP32)
        usum = sb("usum", [P, 2], FP32)
        ut = sb("ut", [P, KT, RANK], FP32)
        gram = sb("gram", [RANK, RANK], FP32)
        ecur = sb("ecur", [P, GB, RANK], FP32)
        ets = sb("ets", [RANK, GT], FP32)
        eg = sb("eg", [P, GB, RANK], FP32)
        var = sb("var", [P, 3, BATCH], FP32)
        w = sb("w", [P, KT, DIM], FP32)
        wt = sb("wt", [P, 4, DIM], FP32)
        wq = sb("wq", [P, KT, DIM], BF16)
        wm = sb("wm", [P, 4], FP32)
        row = sb("row", [1, P], FP32)
        ones = sb("ones", [1, P], FP32)
        p_ut = pb("p_ut", [P, 512], FP32)
        p_g = pb("p_g", [P, 512], FP32)
        p_et = pb("p_et", [P, 512], FP32)
        p_eg = pb("p_eg", [P, 512], FP32)
        p_w = pb("p_w", [P, 512], FP32)

        ids_in, u_in, const_in, w_in = sem("ids_in"), sem("u_in"), sem("const_in"), sem("w_in")
        ident_ok, idx_ok, gathered = sem("ident_ok"), sem("idx_ok"), sem("gathered")
        u_centred, ut_done, ut_sb, g_done, g_sb = (sem(n) for n in ("u_centred", "ut_done", "ut_sb", "g_done", "g_sb"))
        ecur_ok, et_done, et_sb, eg_done = sem("ecur_ok"), sem("et_done"), sem("et_sb"), sem("eg_done")
        a_exp, var_ok, std_ok = sem("a_exp"), sem("var_ok"), sem("std_ok")
        wm_ok, wrow_done, wmax_ok, wbc_done, ones_ok = (sem(n) for n in ("wm_ok", "wrow_done", "wmax_ok", "wbc_done", "ones_ok"))
        wq_ok, wq_out, dve_chain, pad_ok = sem("wq_ok"), sem("wq_out"), sem("dve_chain"), sem("pad_ok")
        block = ctx.enter_context(nc.Block())

        @block.sync
        def _(sp):
            sp.dma_start(ids[:, :], d["x"]).then_inc(ids_in, 16)
            sp.dma_start(s["upk"][0:RANK, :], d["lora_up"]).then_inc(u_in, 16)
            sp.dma_start(s["upk"][U0:U0 + RANK, :], d["lora_up"]).then_inc(u_in, 16)
            sp.dma_start(araw[:, :, :], d["A_log"].rearrange("(k p) n -> p k n", p=P)).then_inc(const_in, 16)
            sp.dma_start(dvec[:, :], d["D"]).then_inc(const_in, 16)
            sp.dma_start(s["dtb"][:, :], d["dt_b"]).then_inc(const_in, 16)
            sp.dma_start(s["xpw"][:, :, :], d["xp_wT"].rearrange("(k p) n -> p k n", p=P)).then_inc(const_in, 16)
            sp.dma_start(s["dtw"][:, :], d["dt_wT"]).then_inc(const_in, 16)
            sp.dma_start(w[:, :, :], d["ffn_wT"].rearrange("(k p) n -> p k n", p=P)).then_inc(w_in, 16)
            sp.wait_ge(wq_ok, KT)
            sp.dma_start(d["wq"].rearrange("(k p) n -> p k n", p=P), wq[:, :, :]).then_inc(wq_out, 16)
            sp.wait_ge(wq_out, 16)
            sp.wait_ge(const_in, 5 * 16)

        @block.gpsimd
        def _(pool):
            nc.gpsimd.memset(s["ident"][:, :], 0.0).then_inc(pad_ok, 1)
            nc.gpsimd.memset(s["etok"][:, :, RANK:U0], 0.0).then_inc(pad_ok, 1)
            pool.wait_ge(pad_ok, 2)
            nc.gpsimd.affine_select(out=s["ident"][:, :], in_=s["ident"][:, :], compare_op=ALU.not_equal, fill=1.0,
                                    base=0, pattern=[[-1, P]], channel_multiplier=1).then_inc(ident_ok, 1)
            pool.wait_ge(idx_ok, 1)
            for b in range(BATCH):
                nc.gpsimd.indirect_dma_start(
                    out=s["etok"][:, b, 0:RANK], out_offset=None, in_=d["lora_down"],
                    in_offset=bass.IndirectOffsetOnAxis(ap=idx[:, b:b + 1], axis=0)).then_inc(gathered, 16)
            pool.wait_ge(gathered, 16 * BATCH)

        @block.scalar
        def _(act):
            act.wait_ge(const_in, 5 * 16)
            nc.scalar.activation(s["aneg"][:, :, :], araw[:, :, :], ACT.Exp).then_inc(a_exp, 1)
            act.wait_ge(var_ok, 1)
            nc.scalar.activation(var[:, 1, :], var[:, 0, :], ACT.Sqrt).then_inc(std_ok, 1)

        @block.tensor
        def _(pe):
            pe.wait_ge(ident_ok, 1)
            pe.wait_ge(u_centred, 1)
            for k in range(KT):
                last = nc.tensor.transpose(p_ut[:, k * RANK:(k + 1) * RANK], s["upk"][U0:U0 + RANK, k * P:(k + 1) * P],
                                           s["ident"][U0:U0 + RANK, U0:U0 + RANK])
            last.then_inc(ut_done, 1)
            pe.wait_ge(ut_sb, 1)
            for k in range(KT):
                last = nc.tensor.matmul(p_g[0:RANK, 0:RANK], ut[:, k, :], ut[:, k, :], start=k == 0, stop=k == KT - 1)
            last.then_inc(g_done, 1)
            pe.wait_ge(wm_ok, 1)
            nc.tensor.transpose(p_w[0:1, 0:P], wm[:, 0:1], s["ident"][:, :]).then_inc(wrow_done, 1)
            pe.wait_ge(wmax_ok, 1)
            pe.wait_ge(ones_ok, 1)
            nc.tensor.matmul(p_w[:, P:P + 1], ones[0:1, :], row[0:1, 0:1], start=True, stop=True).then_inc(wbc_done, 1)
            pe.wait_ge(g_sb, 1)
            with nc.tensor.Fori(0, GROUPS) as g:
                pe.wait_ge(ecur_ok, g + 1)
                for b in range(GB):
                    last = nc.tensor.transpose(p_et[0:RANK, b * P:(b + 1) * P], ecur[:, b, :], s["ident"][:, :])
                last.then_inc(et_done, 1)
                pe.wait_ge(et_sb, g + 1)
                for b in range(GB):
                    last = nc.tensor.matmul(p_eg[:, b * RANK:(b + 1) * RANK], ets[:, b * P:(b + 1) * P], gram[:, :],
                                            start=True, stop=True)
                last.then_inc(eg_done, 1)

        @block.vector
        def _(dve):
            chain = [0]

            def link(ins):
                chain[0] += 1
                ins.then_inc(dve_chain, 1)
                dve.wait_ge(dve_chain, chain[0])

            dve.wait_ge(ids_in, 16)
            link(nc.vector.tensor_copy(idf[:, 0, :], ids[:, :]))
            link(nc.vector.tensor_scalar(idf[:, 1, :], idf[:, 0, :], 0.0, float(VOCAB), ALU.is_lt, ALU.mult))
            link(nc.vector.tensor_tensor(idf[:, 2, :], idf[:, 0, :], idf[:, 1, :], ALU.add))
            nc.vector.tensor_scalar(idx[:, :], idf[:, 2, :], 0.0, float(VOCAB - 1), ALU.max, ALU.min).then_inc(idx_ok, 1)
            dve.wait_ge(u_in, 32)
            uc = s["upk"][U0:U0 + RANK, :]
            link(nc.vector.reduce_sum(usum[U0:U0 + RANK, 0:1], uc, axis=AX.X))
            link(nc.vector.tensor_scalar(usum[U0:U0 + RANK, 1:2], usum[U0:U0 + RANK, 0:1], -1.0 / DIM, None, ALU.mult))
            nc.vector.tensor_scalar(uc, uc, usum[U0:U0 + RANK, 1:2], None, ALU.add).then_inc(u_centred, 1)
            dve.wait_ge(ut_done, 1)
            nc.vector.tensor_copy(ut[:, :, :], p_ut[:, 0:KT * RANK].rearrange("p (k n) -> p k n", k=KT)).then_inc(ut_sb, 1)
            dve.wait_ge(g_done, 1)
            nc.vector.tensor_scalar(gram[:, :], p_g[0:RANK, 0:RANK], 1.0 / DIM, None, ALU.mult).then_inc(g_sb, 1)
            dve.wait_ge(a_exp, 1)
            nc.vector.tensor_scalar(s["aneg"][:, :, :], s["aneg"][:, :, :], -1.0, None, ALU.mult)
            dve.wait_ge(ident_ok, 1)
            dve.wait_ge(const_in, 5 * 16)
            for k in range(KT):
                nc.vector.tensor_scalar(s["diag"][:, k, :], s["ident"][:, :], dvec[:, k:k + 1], None, ALU.mult)
            nc.vector.memset(ones[:, :], 1.0).then_inc(ones_ok, 1)
            dve.wait_ge(w_in, 16)
            nc.vector.tensor_reduce(wm[:, 0:1], w[:, :, :], AX.XY, ALU.max, apply_absolute_value=True).then_inc(wm_ok, 1)
            dve.wait_ge(wrow_done, 1)
            nc.vector.reduce_max(row[0:1, 0:1], p_w[0:1, 0:P], axis=AX.X).then_inc(wmax_ok, 1)
            dve.wait_ge(wbc_done, 1)
            link(nc.vector.tensor_scalar(s["winv"][:, :], p_w[:, P:P + 1], 1e-12, 1.0 / FP8_MAX, ALU.max, ALU.mult))
            link(nc.vector.reciprocal(wm[:, 1:2], s["winv"][:, :]))
            for k in range(KT):
                link(nc.vector.tensor_scalar(wt[:, 0, :], w[:, k, :], wm[:, 1:2], None, ALU.mult))
                link(nc.vector.tensor_scalar(wt[:, 1, :].bitcast(I32), wt[:, 0, :].bitcast(I32), EXP_BITS, None, ALU.bitwise_and))
                link(nc.vector.tensor_scalar(wt[:, 2, :], wt[:, 1, :], MIN_NORMAL, ROUND, ALU.max, ALU.mult))
                link(nc.vector.tensor_tensor(wt[:, 3, :], wt[:, 0, :], wt[:, 2, :], ALU.add))
                nc.vector.tensor_tensor(wq[:, k, :], wt[:, 3, :], wt[:, 2, :], ALU.subtract).then_inc(wq_ok, 1)
            dve.wait_ge(gathered, 16 * BATCH)
            with nc.vector.Fori(0, GROUPS) as g:
                nc.vector.tensor_copy(ecur[:, :, :], s["etok"][:, bass.ds(g * GB, GB), 0:RANK]).then_inc(ecur_ok, 1)
                dve.wait_ge(et_done, g + 1)
                nc.vector.tensor_copy(ets[:, :], p_et[0:RANK, :]).then_inc(et_sb, 1)
                dve.wait_ge(eg_done, g + 1)
                nc.vector.tensor_tensor(eg[:, :, :], p_eg[:, 0:GB * RANK].rearrange("p (b n) -> p b n", b=GB),
                                        ecur[:, :, :], ALU.mult).then_inc(dve_chain, 1)
                dve.wait_ge(dve_chain, g * 2 + (chain[0] + 1))
                nc.vector.reduce_sum(var[:, 0, bass.ds(g * GB, GB)], eg[:, :, :], axis=AX.X).then_inc(dve_chain, 1)
                dve.wait_ge(dve_chain, g * 2 + (chain[0] + 2))
            chain[0] += 2 * GROUPS
            nc.vector.tensor_scalar(var[:, 0, :], var[:, 0, :], 0.0, EPS, ALU.max, ALU.add).then_inc(var_ok, 1)
            dve.wait_ge(std_ok, 1)
            link(nc.vector.reciprocal(var[:, 2, :], var[:, 1, :]))
            link(nc.vector.tensor_tensor(s["etok"][:, :, U0:U0 + RANK], s["etok"][:, :, 0:RANK],
                                         var[:, 2, :].unsqueeze(2).to_broadcast([P, BATCH, RANK]), ALU.mult))


def scan_stage(nc, d, s):
    with ExitStack() as ctx:
        sb = lambda name, shape, dt: ctx.enter_context(nc.sbuf_tensor(name, shape, dt))
        pb = lambda name, shape, dt: ctx.enter_context(nc.psum_tensor(name, shape, dt))
        sem = lambda name: ctx.enter_context(nc.semaphore(name))
        ecur = sb("ecur2", [P, GB, P], FP32)
        et = sb("et", [U0 + RANK, GT], FP32)
        xt = sb("xt", [P, KT, GT], FP32)
        xpt = sb("xpt", [P, GT], FP32)
        bnext = sb("bnext", [P, GB, STATE], FP32)
        bcur = sb("bcur", [P, GB, STATE], FP32)
        cbc = sb("cbc", [P, STATE, GT], FP32)
        zb = sb("zb", [P, 2, GT], FP32)
        ez = sb("ez", [P, 2, GT], FP32)
        m30 = sb("m30", [P, 1], FP32)
        ux = sb("ux", [P, 2, GT], FP32)
        dtt = sb("dtt", [P, 2, HT, GT], FP32)
        ut = sb("u_tok", [P, 2, GB, HD], FP32)
        v = sb("v", [P, 2, GB, HD], FP32)
        da = sb("da", [P, NDA, 2, GT], FP32)
        hs = sb("hs", [P, NH, 2 * GT], FP32)
        ps = sb("ps", [P, NP, 2, GT], FP32)
        h2t = sb("h2t", [P, HT, GT], FP32)
        h2o = sb("h2o", [P, 2, 2, HD], FP32)
        slot = pb("slot", [P, 2, 2 * GT], FP32)
        yp = pb("yp", [P, HT, GT], FP32)

        names = ("da_ready v_ready slot_full slot_read p_ready r_done y_read ecur_ready zmin_ready e_ready "
                 "sp_ready dt_ready ux_ready bcur_ready h2_stored c_stored h2o_ready zero_ok").split()
        (da_ready, v_ready, slot_full, slot_read, p_ready, r_done, y_read, ecur_ready, zmin_ready, e_ready,
         sp_ready, dt_ready, ux_ready, bcur_ready, h2_stored0, c_stored, h2o_ready, zero_ok) = (sem(n) for n in names)
        h2_stored = [h2_stored0, sem("h2_stored1")]
        m30_ok = sem("m30_ok")
        pads_ok = sem("pads_ok")
        c_loaded = [sem(f"c_loaded{c}") for c in range(4)]
        block = ctx.enter_context(nc.Block())
        h2v = d["h2"].rearrange("(b p) c -> p b c", p=P)
        ident = s["ident"]

        def prep_slot(g, h, kind, arg):
            if isinstance(g, int) and g < 0:
                return PROLOGUE.index((kind, arg)), PROLOGUE.index((kind, arg)) % 2
            return slot_no(g, h, kind, arg), slot_side(g, h, kind, arg)

        def jobs(h, u, last):
            got = PREP_AT[h].get(u, [])
            return [] if last and h == 1 else got

        def z_no(g, h, q):
            return q if isinstance(g, int) and g < 0 else g * 4 + (2 + 2 * h + q)

        def unit_no(g, h, u):
            return g * (2 * UNITS) + (h * UNITS + u)

        def back(g, h, u, n):
            u -= n
            if u < 0:
                u += UNITS
                g, h = (g - 1, 1) if h == 0 else (g, 0)
            if isinstance(g, int) and g < 0:
                return None
            return g, h, u

        def groups(engine, body):
            body(0, False)
            with engine.Fori(1, GROUPS - 1) as g:
                body(g, False)
            body(GROUPS - 1, True)

        @block.sync
        def _(sp):
            def c_job(g, ahead):
                no, _ = prep_slot(g, 1, "P", 0)
                sp.wait_ge(slot_read, no + 1)
                sp.dma_start(d["c"][bass.ds(ahead, 1), :, :].rearrange("o n t -> (o n) t"),
                             xpt[DTR + STATE:XP, :]).then_inc(c_stored, 16)
                sp.wait_ge(c_stored, ahead * 16 + 16)
                for c in range(4):
                    if not (isinstance(g, int) and g < 0):
                        sp.wait_ge(p_ready, unit_no(g, 1, 8 * c + 7) + 1)
                    sp.dma_start(cbc[:, 4 * c:4 * c + 4, :],
                                 d["c"][bass.ds(ahead, 1), 4 * c:4 * c + 4, :].rearrange("o n t -> o (n t)")
                                 .to_broadcast([P, 4 * GT])).then_inc(c_loaded[c], 16)

            def h2_job(g, h, gp, hp):
                for bp in range(2):
                    fno = (gp * 2 + hp) * 2 + bp
                    sp.wait_ge(h2o_ready, fno * 2 + 2)
                    sp.dma_start(h2v[:, bass.ds(gp * GB + 2 * bp, 2), hp * HD:(hp + 1) * HD],
                                 h2o[:, bp, :, :]).then_inc(h2_stored[bp], 16)

            def body(g, last):
                if not (isinstance(g, int) and g == 0):
                    h2_job(g, 0, g - 1, 1)
                h2_job(g, 1, g, 0)
                if not last:
                    c_job(g, g + 1)

            c_job(-1, 0)
            groups(nc.sync, body)
            h2_job(GROUPS, 0, GROUPS - 1, 1)
            for bp in range(2):
                sp.wait_ge(h2_stored[bp], 16 * 2 * GROUPS)

        @block.gpsimd
        def _(pool):
            def ecur_job(g, ahead):
                if not (isinstance(g, int) and g < 0):
                    if isinstance(g, int) and g == 0:
                        pool.wait_ge(slot_full, PROLOGUE.index(("E", 1)) + 1)
                    else:
                        pool.wait_ge(slot_full, slot_no(g - 1, 1, "E", 1) + 1)
                nc.gpsimd.tensor_copy(ecur[:, :, 0:U0 + RANK], s["etok"][:, bass.ds(ahead * GB, GB), :]).then_inc(ecur_ready, 1)

            def zmin_job(g, h, q):
                if static(g, -1):
                    pool.wait_ge(slot_read, PROLOGUE.index(("Z", q)) + 1)
                nc.gpsimd.tensor_scalar(ez[:, :, :], zb[:, :, :], 30.0, -3.0e38, ALU.min, ALU.max).then_inc(zmin_ready, 1)

            def dt_job(g, h, q, hn):
                z = z_no(g, h, q)
                pool.wait_ge(sp_ready, z + 1)
                nc.gpsimd.tensor_tensor(dtt[:, hn, 2 * q:2 * q + 2, :], zb[:, :, :], ez[:, :, :], ALU.add).then_inc(dt_ready, 1)
                pool.wait_ge(dt_ready, z + 1)
                if q == 1:
                    pool.wait_ge(slot_full, prep_slot(g, h, "U", 0)[0] + 1)
                elif static(g, 0) and h == 0:
                    pool.wait_ge(slot_full, PROLOGUE.index(("U", 1)) + 1)
                elif not static(g, -1):
                    gb, hb = (g - 1, 1) if h == 0 else (g, 0)
                    pool.wait_ge(slot_full, slot_no(gb, hb, "U", 1) + 1)
                k = hn * HT + 2 * q
                nc.gpsimd.tensor_tensor(ux[:, :, :], dtt[:, hn, 2 * q:2 * q + 2, :], xt[:, k:k + 2, :],
                                        ALU.mult).then_inc(ux_ready, 1)

            def cmul(g, h, u):
                n, q = u // 2, u % 2
                sno = slot_no(g, h, "S", u)
                if n % 4 == 0 and q == 0 and h == 0:
                    pool.wait_ge(c_loaded[n // 4], g * 16 + 16)
                pool.wait_ge(slot_read, sno + 1)
                b = back(g, h, u, NP)
                if b:
                    pool.wait_ge(r_done, unit_no(*b) + 1)
                nc.gpsimd.tensor_tensor(ps[:, u % NP, :, :], hs[:, u % NH, :].rearrange("p (j t) -> p j t", j=2),
                                        cbc[:, n:n + 1, :].to_broadcast([P, 2, GT]), ALU.mult).then_inc(p_ready, 1)

            def body(g, last):
                for h in range(2):
                    for u in range(UNITS):
                        cmul(g, h, u)
                        if last and h == 1:
                            continue
                        if h == 1 and u == 2:
                            ecur_job(g, g + 1)
                        for q in range(2):
                            if u == Z_AT[h][q] + 1:
                                zmin_job(g, h, q)
                            if u == Z_AT[h][q] + DT_AFTER:
                                dt_job(g, h, q, 1 - h)

            ecur_job(-1, 0)
            for q in range(2):
                zmin_job(-1, 1, q)
                dt_job(-1, 1, q, 0)
            groups(nc.gpsimd, body)

        @block.scalar
        def _(act):
            def softplus_job(g, h, q):
                z = z_no(g, h, q)
                act.wait_ge(zmin_ready, z + 1)
                nc.scalar.activation(ez[:, :, :], ez[:, :, :], ACT.Exp).then_inc(e_ready, 1)
                nc.scalar.activation(zb[:, :, :], zb[:, :, :], ACT.Relu, bias=m30[:, :])
                act.wait_ge(e_ready, z + 1)
                nc.scalar.activation(ez[:, :, :], ez[:, :, :], ACT.Ln, bias=1.0).then_inc(sp_ready, 1)

            def b_mul(g, h, n):
                b = back(g, h, 2 * n, 4)
                if b:
                    act.wait_ge(slot_full, slot_no(b[0], b[1], "S", b[2] + 1) + 1)
                for i in range(GB):
                    m = nc.scalar.activation(v[:, n % 2, i, :], ut[:, h, i, :], ACT.Copy, scale=bcur[:, i, n:n + 1])
                m.then_inc(v_ready, 1)

            def exp_a(g, h, u):
                n, q = u // 2, u % 2
                b = back(g, h, u, NDA)
                if b:
                    act.wait_ge(slot_read, slot_no(b[0], b[1], "S", b[2]) + 1)
                for j in range(2):
                    t = 2 * q + j
                    m = nc.scalar.activation(
                        da[:, u % NDA, j, :].rearrange("p (b t) -> p b t", b=GB)[:, :, 1:SEQ],
                        dtt[:, h, t, :].rearrange("p (b t) -> p b t", b=GB)[:, :, 1:SEQ],
                        ACT.Exp, scale=s["aneg"][:, h * HT + t, n:n + 1])
                m.then_inc(da_ready, 1)

            def body(g, last):
                for h in range(2):
                    if h == 0:
                        no = slot_no(g - 1, 1, "B", 0) if not isinstance(g, int) or g > 0 else PROLOGUE.index(("B", 0))
                        act.wait_ge(slot_read, no + 1)
                        if not static(g, 0):
                            act.wait_ge(v_ready, g * (2 * STATE))
                        nc.scalar.activation(bcur[:, :, :], bnext[:, :, :], ACT.Copy).then_inc(bcur_ready, 1)
                        act.wait_ge(bcur_ready, g + 1)
                    if h == 1:
                        no = slot_no(g, 0, "U", 1)
                    else:
                        no = slot_no(g - 1, 1, "U", 1) if not isinstance(g, int) or g > 0 else PROLOGUE.index(("U", 1))
                    act.wait_ge(slot_read, no + 1)
                    for u in range(UNITS):
                        if u % 2 == 0:
                            b_mul(g, h, u // 2)
                        exp_a(g, h, u)
                        if last and h == 1:
                            continue
                        for q in range(2):
                            if u == Z_AT[h][q] + ACT_AFTER:
                                softplus_job(g, h, q)

            act.wait_ge(m30_ok, 1)
            for q in range(2):
                softplus_job(-1, 1, q)
            act.wait_ge(zero_ok, 1)
            groups(nc.scalar, body)

        @block.tensor
        def _(pe):
            def free_slot(no):
                if isinstance(no, int) and no < 2:
                    return
                pe.wait_ge(slot_read, no - 1)

            def trans(g, h, u):
                n, q = u // 2, u % 2
                no, side = slot_no(g, h, "S", u), slot_side(g, h, "S", u)
                free_slot(no)
                if q == 0:
                    pe.wait_ge(v_ready, g * (2 * STATE) + (h * STATE + n + 1))
                for j in range(2):
                    for b in range(GB):
                        m = nc.tensor.transpose(slot[:, side, j * GT + b * P:j * GT + (b + 1) * P],
                                                v[:, n % 2, b, (2 * q + j) * P:(2 * q + j + 1) * P], ident[:, :])
                m.then_inc(slot_full, 1)

            def reduce_n(g, h, u):
                n, q = u // 2, u % 2
                pe.wait_ge(p_ready, unit_no(g, h, u) + 1)
                for j in range(2):
                    m = nc.tensor.matmul(yp[:, 2 * q + j, :], ident[:, :], ps[:, u % NP, j, :],
                                         start=False, stop=n == STATE - 1)
                m.then_inc(r_done, 1)

            def residual(g, h, q):
                if not (isinstance(g, int) and g == 0 and h == 0):
                    pe.wait_ge(y_read, g * 4 + (2 * h + q - 1))
                for j in range(2):
                    k = h * HT + 2 * q + j
                    nc.tensor.matmul(yp[:, 2 * q + j, :], s["upk"][0:RANK, k * P:(k + 1) * P], et[0:RANK, :],
                                     start=True, stop=False)

            def d_x(g, h, q):
                for j in range(2):
                    k = h * HT + 2 * q + j
                    nc.tensor.matmul(yp[:, 2 * q + j, :], s["diag"][:, k, :], xt[:, k, :], start=False, stop=False)

            def h2_trans(no, side, bp, yno):
                free_slot(no)
                pe.wait_ge(y_read, yno)
                for b in range(2):
                    for t in range(HT):
                        m = nc.tensor.transpose(slot[:, side, b * HD + t * P:b * HD + (t + 1) * P],
                                                h2t[:, t, (2 * bp + b) * P:(2 * bp + b + 1) * P], ident[:, :])
                m.then_inc(slot_full, 1)

            def prep(g, h, kind, arg, ahead):
                no, side = prep_slot(g, h, kind, arg)
                free_slot(no)
                if kind == "E":
                    if arg == 0:
                        pe.wait_ge(ecur_ready, ahead + 1)
                    for b in range(2):
                        m = nc.tensor.transpose(slot[:, side, b * P:(b + 1) * P], ecur[:, 2 * arg + b, :], ident[:, :])
                if kind == "X":
                    if arg == 0:
                        pe.wait_ge(slot_read, prep_slot(g, h, "E", 1)[0] + 1)
                    for j in range(2):
                        k = 2 * arg + j
                        m = nc.tensor.matmul(slot[:, side, j * GT:(j + 1) * GT], s["upk"][U0:U0 + RANK, k * P:(k + 1) * P],
                                             et[U0:U0 + RANK, :], start=True, stop=True)
                if kind == "P":
                    pe.wait_ge(slot_read, prep_slot(g, h, "X", 3)[0] + 1)
                    for k in range(KT):
                        m = nc.tensor.matmul(slot[0:XP, side, 0:GT], s["xpw"][:, k, :], xt[:, k, :],
                                             start=k == 0, stop=k == KT - 1)
                if kind in "BZ":
                    pno = prep_slot(g, h, "P", 0)[0] if h == 1 else None
                    if pno is not None:
                        pe.wait_ge(slot_read, pno + 1)
                if kind == "B":
                    for b in range(GB):
                        m = nc.tensor.transpose(slot[:, side, b * P:(b + 1) * P], xpt[:, b * P:(b + 1) * P], ident[:, :])
                if kind == "Z":
                    for j in range(2):
                        k = (1 - h) * HT + 2 * arg + j
                        m = nc.tensor.matmul(slot[:, side, j * GT:(j + 1) * GT], s["dtw"][:, k * P:(k + 1) * P],
                                             xpt[0:DTR, :], start=True, stop=True)
                if kind == "U":
                    pe.wait_ge(ux_ready, z_no(g, h, arg) + 1)
                    for b in range(GB):
                        for j in range(2):
                            m = nc.tensor.transpose(slot[:, side, (b * 2 + j) * P:(b * 2 + j + 1) * P],
                                                    ux[:, j, b * P:(b + 1) * P], ident[:, :])
                m.then_inc(slot_full, 1)

            def body(g, last):
                for h in range(2):
                    first = isinstance(g, int) and g == 0 and h == 0
                    for u in range(UNITS):
                        trans(g, h, u)
                        if u in (LAG, LAG + 1):
                            residual(g, h, u - LAG)
                        b = back(g, h, u, LAG)
                        if b:
                            reduce_n(*b)
                        if u in DX_AT:
                            d_x(g, h, DX_AT[u])
                        if u == F_AT and not first:
                            for bp in range(2):
                                h2_trans(slot_no(g, h, "F", bp), slot_side(g, h, "F", bp), bp, g * 4 + 2 * h)
                        for kind, arg in jobs(h, u, last):
                            prep(g, h, kind, arg, g + 1)

            pe.wait_ge(pads_ok, 1)
            for kind, arg in PROLOGUE:
                prep(-1, 1, kind, arg, 0)
            groups(nc.tensor, body)
            for u in range(UNITS - LAG, UNITS):
                reduce_n(GROUPS - 1, 1, u)
            for bp in range(2):
                no, side = TAIL + bp, bp
                h2_trans(no, side, bp, 4 * GROUPS)

        @block.vector
        def _(dve):
            def scan(g, h, u):
                no, side = slot_no(g, h, "S", u), slot_side(g, h, "S", u)
                dve.wait_ge(da_ready, unit_no(g, h, u) + 1)
                dve.wait_ge(slot_full, no + 1)
                b = back(g, h, u, NH)
                if b:
                    dve.wait_ge(p_ready, unit_no(*b) + 1)
                nc.vector.tensor_tensor_scan(hs[:, u % NH, :], da[:, u % NDA, :, :].rearrange("p j t -> p (j t)"),
                                             slot[:, side, :], 0.0, ALU.mult, ALU.add).then_inc(slot_read, 1)

            def y_out(g, h, q):
                dve.wait_ge(r_done, unit_no(g, h, UNITS - 2 + q) + 1)
                nc.vector.tensor_copy(h2t[:, 2 * q:2 * q + 2, :], yp[:, 2 * q:2 * q + 2, :]).then_inc(y_read, 1)

            def h2_out(no, side, bp, g, h):
                dve.wait_ge(slot_full, no + 1)
                blk = g * 2 + h
                if not (isinstance(blk, int) and blk == 0):
                    dve.wait_ge(h2_stored[bp], blk * 16)
                tile = g * GB + 2 * bp
                for b in range(2):
                    part = slot[:, side, b * HD:(b + 1) * HD]
                    nc.vector.bn_stats(s["stats"][:, bass.ds(tile + b, 1), h, :].rearrange("p o f -> p (o f)"), part)
                    nc.vector.tensor_scalar(h2o[:, bp, b, :], part, 1.0, None, ALU.mult, ALU.max,
                                            accum_out=s["hmax"][:, bass.ds(tile + b, 1), h]).then_inc(h2o_ready, 1)
                nc.vector.tensor_reduce(s["hmin"][:, bass.ds(tile, 2), h],
                                        slot[:, side, :].rearrange("p (b c) -> p b c", b=2), AX.X, ALU.min).then_inc(slot_read, 1)

            def prep(g, h, kind, arg, ahead):
                no, side = prep_slot(g, h, kind, arg)
                dve.wait_ge(slot_full, no + 1)
                if kind == "E":
                    m = nc.vector.tensor_copy(et[:, arg * 2 * P:(arg + 1) * 2 * P], slot[0:U0 + RANK, side, 0:2 * P])
                if kind == "X":
                    m = nc.vector.tensor_copy(xt[:, 2 * arg:2 * arg + 2, :],
                                              slot[:, side, :].rearrange("p (j t) -> p j t", j=2))
                if kind == "P":
                    if not (isinstance(g, int) and g < 0):
                        dve.wait_ge(c_stored, ahead * 16)
                    m = nc.vector.tensor_copy(xpt[0:XP, :], slot[0:XP, side, 0:GT])
                if kind == "B":
                    if not (isinstance(g, int) and g < 0):
                        dve.wait_ge(bcur_ready, ahead)
                    m = nc.vector.tensor_copy(bnext[:, :, :], slot[:, side, 0:GT].rearrange("p (b n) -> p b n", b=GB)
                                              [:, :, DTR:DTR + STATE])
                if kind == "Z":
                    z = z_no(g, h, arg)
                    if not (isinstance(z, int) and z == 0):
                        dve.wait_ge(dt_ready, z)
                    for j in range(2):
                        k = (1 - h) * HT + 2 * arg + j
                        m = nc.vector.tensor_scalar(zb[:, j, :], slot[:, side, j * GT:(j + 1) * GT],
                                                    s["dtb"][:, k:k + 1], None, ALU.add)
                if kind == "U":
                    m = nc.vector.tensor_copy(ut[:, 1 - h, :, arg * 2 * P:(arg + 1) * 2 * P],
                                              slot[:, side, :].rearrange("p (b c) -> p b c", b=GB))
                m.then_inc(slot_read, 1)

            def body(g, last):
                for h in range(2):
                    first = isinstance(g, int) and g == 0 and h == 0
                    gp, hp = (g - 1, 1) if h == 0 else (g, 0)
                    for u in range(UNITS):
                        scan(g, h, u)
                        if not first and u in (LAG - 2, LAG - 1):
                            y_out(gp, hp, u - (LAG - 2))
                        if u == F_AT and not first:
                            for bp in range(2):
                                h2_out(slot_no(g, h, "F", bp), slot_side(g, h, "F", bp), bp, gp, hp)
                        for kind, arg in jobs(h, u, last):
                            prep(g, h, kind, arg, g + 1)

            nc.vector.memset(xpt[XP:P, :], 0.0)
            nc.vector.memset(ecur[:, :, U0 + RANK:P], 0.0).then_inc(pads_ok, 1)
            nc.vector.memset(m30[:, :], -30.0).then_inc(m30_ok, 1)
            for c in range(NDA):
                z0 = nc.vector.memset(da[:, c, :, :].rearrange("p j (b t) -> p (j b) t", t=SEQ)[:, :, 0:1], 0.0)
            z0.then_inc(zero_ok, 1)
            for kind, arg in PROLOGUE:
                prep(-1, 1, kind, arg, 0)
            groups(nc.vector, body)
            for q in range(2):
                y_out(GROUPS - 1, 1, q)
            for bp in range(2):
                h2_out(TAIL + bp, bp, bp, GROUPS - 1, 1)


def ffn_stage(nc, d, s):
    with ExitStack() as ctx:
        sb = lambda name, shape, dt: ctx.enter_context(nc.sbuf_tensor(name, shape, dt))
        pb = lambda name, shape, dt: ctx.enter_context(nc.psum_tensor(name, shape, dt))
        sem = lambda name: ctx.enter_context(nc.semaphore(name))
        UN = 4
        TURNS = BATCH // UN
        ms = sb("ms", [P, 4, BATCH], FP32)
        dev = sb("dev", [P, BATCH, 4], FP32)
        mean = sb("mean", [P, BATCH], FP32)
        std = sb("std", [P, BATCH], FP32)
        rstd = sb("rstd", [P, BATCH], FP32)
        ext = sb("ext", [P, 2, BATCH], FP32)
        sc = sb("sc", [P, BATCH], FP32)
        nb = sb("nb", [P, BATCH], FP32)
        cm = sb("cm", [P, 4], FP32)
        row = sb("row2", [1, P], FP32)
        ones = sb("ones2", [1, P], FP32)
        identb = sb("identb", [P, P], BF16)
        wq = sb("wq2", [P, KT, DIM], BF16)
        bias = sb("bias", [P, DIM], FP32)
        h2 = sb("h2_in", [P, UN, DIM], FP32)
        hb = sb("hb", [P, 2, DIM], FP32)
        v = sb("v2", [P, 2, DIM], FP32)
        e = sb("e2", [P, DIM], FP32)
        m = sb("m2", [P, DIM], FP32)
        w = sb("w2", [P, DIM], FP32)
        q = sb("q2", [P, 2, DIM], BF16)
        qt = sb("qt", [P, 2, KT, P], BF16)
        o = sb("o", [P, 2, DIM], FP32)
        p_m = pb("p_m", [P, 512], FP32)
        qp = pb("qp", [P, 2, KT * P], BF16)
        acc = pb("acc", [P, 2, DIM], FP32)
        names = ("w_in bias_in var_ok std_ok cm_ok row_done max_ok bc_done ones_ok scale_ok dve_chain h2_used "
                 "v_ready hb_ready q_ready qp_ready qt_ready acc_ready o_ready").split()
        (w_in, bias_in, var_ok, std_ok, cm_ok, row_done, max_ok, bc_done, ones_ok, scale_ok, dve_chain, _,
         v_ready, hb_ready, q_ready, qp_ready, qt_ready, acc_ready, o_ready) = (sem("f_" + n) for n in names)
        h2_in = [sem(f"f_h2_in{j}") for j in range(UN)]
        o_out = [sem(f"f_o_out{j}") for j in range(2)]
        block = ctx.enter_context(nc.Block())
        h2v = d["h2"].rearrange("(b p) c -> p b c", p=P)
        ov = d["out"].rearrange("(b p) c -> p b c", p=P)

        def turns(engine, body):
            body(0)
            with engine.Fori(1, TURNS) as i:
                body(i)

        @block.sync
        def _(sp):
            sp.dma_start(wq[:, :, :], d["wq"].rearrange("(k p) n -> p k n", p=P)).then_inc(w_in, 16)
            sp.dma_start(bias[:, :], d["ffn_b"].to_broadcast([P, DIM])).then_inc(bias_in, 16)

            def body(i):
                for j in range(UN):
                    if not static(i, 0):
                        sp.wait_ge(v_ready, i * UN + (j - UN + 1))
                        sp.wait_ge(hb_ready, i * UN + (j - UN + 1))
                    sp.dma_start(h2[:, j, :], h2v[:, bass.ds(i * UN + j, 1), :].rearrange("p o c -> p (o c)")).then_inc(h2_in[j], 16)

            turns(nc.sync, body)

        @block.gpsimd
        def _(pool):
            pool.wait_ge(bias_in, 16)

            def body(i):
                for j in range(UN):
                    pool.wait_ge(h2_in[j], i * 16 + 16)
                    if not (static(i, 0) and j < 2):
                        pool.wait_ge(o_ready, i * UN + (j - 1))
                    nc.gpsimd.tensor_tensor(hb[:, j % 2, :], h2[:, j, :], bias[:, :], ALU.add).then_inc(hb_ready, 1)

            turns(nc.gpsimd, body)

        @block.scalar
        def _(act):
            act.wait_ge(var_ok, 1)
            nc.scalar.activation(std[:, :], ms[:, 1, :], ACT.Sqrt).then_inc(std_ok, 1)
            act.wait_ge(scale_ok, 1)

            def store(i, j):
                act.wait_ge(o_ready, i * UN + (j + 1))
                act.dma_start(ov[:, bass.ds(i * UN + j, 1), :].rearrange("p o c -> p (o c)"), o[:, j % 2, :]).then_inc(o_out[j % 2], 16)

            def body(i):
                for j in range(UN):
                    act.wait_ge(h2_in[j], i * 16 + 16)
                    if not (static(i, 0) and j < 2):
                        act.wait_ge(q_ready, i * UN + (j - 1))
                    nc.scalar.activation(v[:, j % 2, :], h2[:, j, :], ACT.Identity, bias=nb[:, bass.ds(i * UN + j, 1)],
                                         scale=sc[:, bass.ds(i * UN + j, 1)]).then_inc(v_ready, 1)
                    if not (static(i, 0) and j == 0):
                        qt_copy(i, j - 1)
                    if not (static(i, 0) and j < 2):
                        store(i, j - 2)

            def qt_copy(i, j):
                act.wait_ge(qp_ready, i * UN + (j + 1))
                if not (static(i, 0) and j < 2):
                    act.wait_ge(acc_ready, i * UN + (j - 1))
                nc.scalar.activation(qt[:, j % 2, :, :], qp[:, j % 2, :].rearrange("p (k t) -> p k t", k=KT),
                                     ACT.Copy).then_inc(qt_ready, 1)

            turns(nc.scalar, body)
            qt_copy(TURNS - 1, UN - 1)
            store(TURNS - 1, UN - 2)
            store(TURNS - 1, UN - 1)
            for j in range(2):
                act.wait_ge(o_out[j], 16 * BATCH // 2)

        @block.tensor
        def _(pe):
            pe.wait_ge(cm_ok, 1)
            nc.tensor.transpose(p_m[0:1, 0:P], cm[:, 0:1], s["ident"][:, :]).then_inc(row_done, 1)
            pe.wait_ge(ones_ok, 1)
            pe.wait_ge(max_ok, 1)
            nc.tensor.matmul(p_m[:, P:P + 1], ones[0:1, :], row[0:1, 0:1], start=True, stop=True).then_inc(bc_done, 1)
            pe.wait_ge(w_in, 16)

            def transposes(i, j):
                pe.wait_ge(q_ready, i * UN + (j + 1))
                if not (static(i, 0) and j < 2):
                    pe.wait_ge(qt_ready, i * UN + (j - 1))
                for k in range(KT):
                    t = nc.tensor.transpose(qp[:, j % 2, k * P:(k + 1) * P], q[:, j % 2, k * P:(k + 1) * P], identb[:, :])
                t.then_inc(qp_ready, 1)

            def products(i, j):
                pe.wait_ge(qt_ready, i * UN + (j + 1))
                if not (static(i, 0) and j < 2):
                    pe.wait_ge(o_ready, i * UN + (j - 1))
                for n in range(2):
                    for k in range(KT):
                        t = nc.tensor.matmul(acc[:, j % 2, n * HD:(n + 1) * HD], qt[:, j % 2, k, :],
                                             wq[:, k, n * HD:(n + 1) * HD], start=k == 0, stop=k == KT - 1)
                t.then_inc(acc_ready, 1)

            def body(i):
                for j in range(UN):
                    transposes(i, j)
                    if not (static(i, 0) and j == 0):
                        products(i, j - 1)

            turns(nc.tensor, body)
            products(TURNS - 1, UN - 1)

        @block.vector
        def _(dve):
            chain = [0]

            def link(ins):
                chain[0] += 1
                ins.then_inc(dve_chain, 1)
                dve.wait_ge(dve_chain, chain[0])

            part = s["stats"][:, :, :, :].rearrange("p b h (a c) -> p b (h a) c", c=3)
            link(nc.vector.reduce_sum(ms[:, 0, :], part[:, :, :, 1], axis=AX.X))
            link(nc.vector.tensor_scalar(mean[:, :], ms[:, 0, :], 0.25, None, ALU.mult))
            link(nc.vector.tensor_tensor(dev[:, :, :], part[:, :, :, 1],
                                         mean[:, :].unsqueeze(2).to_broadcast([P, BATCH, 4]), ALU.subtract))
            link(nc.vector.tensor_tensor(dev[:, :, :], dev[:, :, :], dev[:, :, :], ALU.mult))
            link(nc.vector.scalar_tensor_tensor(dev[:, :, :], dev[:, :, :], DIM / 4.0, part[:, :, :, 2], ALU.mult, ALU.add))
            link(nc.vector.reduce_sum(ms[:, 0, :], dev[:, :, :], axis=AX.X))
            nc.vector.tensor_scalar(ms[:, 1, :], ms[:, 0, :], 1.0 / DIM, EPS, ALU.mult, ALU.add).then_inc(var_ok, 1)
            dve.wait_ge(std_ok, 1)
            link(nc.vector.reciprocal(rstd[:, :], std[:, :]))
            link(nc.vector.tensor_tensor(ext[:, 0, :], s["hmax"][:, :, 0], s["hmax"][:, :, 1], ALU.max))
            link(nc.vector.tensor_tensor(ext[:, 1, :], s["hmin"][:, :, 0], s["hmin"][:, :, 1], ALU.min))
            link(nc.vector.tensor_tensor(ext[:, 0, :], ext[:, 0, :], mean[:, :], ALU.subtract))
            link(nc.vector.tensor_tensor(ext[:, 1, :], mean[:, :], ext[:, 1, :], ALU.subtract))
            link(nc.vector.tensor_tensor(ext[:, 0, :], ext[:, 0, :], ext[:, 1, :], ALU.max))
            link(nc.vector.tensor_tensor(ext[:, 0, :], ext[:, 0, :], rstd[:, :], ALU.mult))
            nc.vector.reduce_max(cm[:, 0:1], ext[:, 0, :], axis=AX.X).then_inc(cm_ok, 1)
            nc.vector.memset(ones[:, :], 1.0).then_inc(ones_ok, 1)
            nc.vector.tensor_copy(identb[:, :], s["ident"][:, :])
            dve.wait_ge(row_done, 1)
            nc.vector.reduce_max(row[0:1, 0:1], p_m[0:1, 0:P], axis=AX.X).then_inc(max_ok, 1)
            dve.wait_ge(bc_done, 1)
            link(nc.vector.tensor_scalar(cm[:, 1:2], p_m[:, P:P + 1], 1e-12, 1.0 / FP8_MAX, ALU.max, ALU.mult))
            link(nc.vector.reciprocal(cm[:, 2:3], cm[:, 1:2]))
            link(nc.vector.tensor_tensor(cm[:, 3:4], cm[:, 1:2], s["winv"][:, :], ALU.mult))
            link(nc.vector.tensor_scalar(sc[:, :], rstd[:, :], cm[:, 2:3], None, ALU.mult))
            nc.vector.scalar_tensor_tensor(nb[:, :], mean[:, :], -1.0, sc[:, :], ALU.mult, ALU.mult).then_inc(scale_ok, 1)

            def round_tile(i, j):
                c = i * (3 * UN) + (chain0 + 3 * j)
                dve.wait_ge(v_ready, i * UN + (j + 1))
                nc.vector.tensor_scalar(e[:, :].bitcast(I32), v[:, j % 2, :].bitcast(I32), EXP_BITS, None,
                                        ALU.bitwise_and).then_inc(dve_chain, 1)
                dve.wait_ge(dve_chain, c + 1)
                nc.vector.tensor_scalar(m[:, :], e[:, :], MIN_NORMAL, ROUND, ALU.max, ALU.mult).then_inc(dve_chain, 1)
                dve.wait_ge(dve_chain, c + 2)
                nc.vector.tensor_tensor(w[:, :], v[:, j % 2, :], m[:, :], ALU.add).then_inc(dve_chain, 1)
                dve.wait_ge(dve_chain, c + 3)
                if not (static(i, 0) and j < 2):
                    dve.wait_ge(qp_ready, i * UN + (j - 1))
                nc.vector.tensor_tensor(q[:, j % 2, :], w[:, :], m[:, :], ALU.subtract).then_inc(q_ready, 1)

            def output(i, j):
                dve.wait_ge(acc_ready, i * UN + (j + 1))
                dve.wait_ge(hb_ready, i * UN + (j + 1))
                if static(i, 0) and j < 2:
                    pass
                elif j < 2:
                    dve.wait_ge(o_out[j % 2], i * 32 + 16 * (j // 2))
                else:
                    dve.wait_ge(o_out[j % 2], i * 32 + 16)
                nc.vector.scalar_tensor_tensor(o[:, j % 2, :], acc[:, j % 2, :], cm[:, 3:4], hb[:, j % 2, :],
                                               ALU.mult, ALU.add).then_inc(o_ready, 1)

            def body(i):
                for j in range(UN):
                    round_tile(i, j)
                    if not (static(i, 0) and j < 2):
                        gi, gj = (i, j - 2) if j >= 2 else (i - 1, j + 2)
                        output(gi, gj)

            chain0 = chain[0]
            turns(nc.vector, body)
            output(TURNS - 1, UN - 2)
            output(TURNS - 1, UN - 1)


def build(nc, d):
    d["h2"] = nc.dram_tensor("h2_scratch", (BATCH * SEQ, DIM), FP32, kind="Internal").ap()
    d["c"] = nc.dram_tensor("c_scratch", (GROUPS, STATE, GT), FP32, kind="Internal").ap()
    d["wq"] = nc.dram_tensor("wq_scratch", (DIM, DIM), BF16, kind="Internal").ap()
    with ExitStack() as ctx:
        s = {}
        for name, shape, dt in (
                ("ident", [P, P], FP32),
                ("winv", [P, 1], FP32),
                ("stats", [P, BATCH, 2, 6], FP32),
                ("hmax", [P, BATCH, 2], FP32),
                ("hmin", [P, BATCH, 2], FP32),
                ("upk", [U0 + RANK, DIM], FP32),
                ("xpw", [P, KT, XP], FP32),
                ("dtw", [DTR, DIM], FP32),
                ("dtb", [P, KT], FP32),
                ("aneg", [P, KT, STATE], FP32),
                ("diag", [P, KT, P], FP32),
                ("etok", [P, BATCH, U0 + RANK], FP32)):
            s[name] = ctx.enter_context(nc.sbuf_tensor("s_" + name, shape, dt))
        setup_stage(nc, d, s)
        scan_stage(nc, d, s)
        ffn_stage(nc, d, s)


def kernel(x, L0_tok_lora_down, L0_tok_lora_up, L0_attn_A_log, L0_attn_D, L0_attn_x_proj_w, L0_attn_dt_proj_w,
           L0_attn_dt_proj_b, L0_ffn_weight, L0_ffn_bias):
    import numpy as np
    import concourse.bacc as bacc
    from concourse.bass_utils import run_bass_kernel_spmd

    arrays = {
        "x": np.ascontiguousarray(np.asarray(x).T),
        "lora_down": np.ascontiguousarray(L0_tok_lora_down),
        "lora_up": np.ascontiguousarray(L0_tok_lora_up),
        "A_log": np.ascontiguousarray(L0_attn_A_log),
        "D": np.ascontiguousarray(np.asarray(L0_attn_D).reshape(KT, P).T),
        "xp_wT": np.ascontiguousarray(np.asarray(L0_attn_x_proj_w).T),
        "dt_wT": np.ascontiguousarray(np.asarray(L0_attn_dt_proj_w).T),
        "dt_b": np.ascontiguousarray(np.asarray(L0_attn_dt_proj_b).reshape(KT, P).T),
        "ffn_wT": np.ascontiguousarray(np.asarray(L0_ffn_weight).T),
        "ffn_b": np.ascontiguousarray(np.asarray(L0_ffn_bias).reshape(1, DIM)),
    }
    nc = bacc.Bacc("TRN2", target_bir_lowering=False, num_devices=1)
    d, feeds = {}, {}
    for name, a in arrays.items():
        feeds["in_" + name] = a
        d[name] = nc.dram_tensor("in_" + name, a.shape, mybir.dt.from_np(a.dtype), kind="ExternalInput").ap()
    out = nc.dram_tensor("out_h", (BATCH * SEQ, DIM), FP32, kind="ExternalOutput")
    d["out"] = out.ap()
    build(nc, d)
    r = run_bass_kernel_spmd(nc, [feeds], core_ids=[0])
    return r.results[0]["out_h"].reshape(BATCH, SEQ, DIM)
```

```python
import concourse.bass as bass
from concourse import mybir
from contextlib import ExitStack

FP32 = mybir.dt.float32
BF16 = mybir.dt.bfloat16
I32 = mybir.dt.int32
U32 = mybir.dt.uint32
ALU = mybir.AluOpType
ACT = mybir.ActivationFunctionType
AX = mybir.AxisListType

P = 128
BATCH, SEQ = 64, 128
VOCAB, RANK = 8000, 16
DIM = 1024
STATE = 16
DTR = 32
XP = DTR + 2 * STATE
KT = DIM // P
GB = 4
GROUPS = BATCH // GB
GT = GB * SEQ
HT = KT // 2
HD = HT * P
STACK = 6 * RANK
UNITS = STATE * 2
EPS = 1e-5
FP8_MAX = 448.0
EXP_BITS = 0x7F800000
MIN_NORMAL = 2.0 ** -6
ROUND = 1.5 * 2.0 ** 20

WEIGHT_PARTS = (0, 1, 2, 0, 1, 0)
W_X = 0
W_Z = W_X + DIM
W_H = W_Z + DIM
W_D = W_H + DIM
W_G = W_D + DIM
W_BC = W_G + RANK
W_COLS = W_BC + 2 * STATE

LAG = 3
NDA, NH, NP = 2, 2, 4
F_AT = 6
PREP_AT = {
    0: {8: [("Z", 0)], 13: [("X", 0)], 14: [("U", 0), ("Z", 1)], 19: [("X", 1)], 20: [("U", 1)]},
    1: {8: [("E", 0)], 9: [("G", 0)], 13: [("R", 0)], 14: [("C", 0)], 15: [("Z", 0)], 20: [("X", 0)],
        21: [("U", 0), ("Z", 1)], 26: [("X", 1)], 27: [("U", 1)]},
}
PROLOGUE = [("E", 0), ("G", 0), ("R", 0), ("C", 0), ("Z", 0), ("X", 0), ("U", 0), ("Z", 1), ("X", 1), ("U", 1)]
GATHER_AT, SPLIT_AT, RSTD_AT = 2, 6, 10
Z_AT = {h: {q: u for u, jobs in PREP_AT[h].items() for kind, q in jobs if kind == "Z"} for h in (0, 1)}
ACT_AFTER, DT_AFTER = 3, 4


def slot_plan(h, final, prep):
    plan = []
    for u in range(UNITS):
        plan.append(("S", u))
        if final and u == F_AT:
            plan += [("F", 0), ("F", 1)]
        if prep:
            plan += PREP_AT[h].get(u, [])
    return plan


PLAN_FIRST = slot_plan(0, False, True)
PLAN = [slot_plan(0, True, True), slot_plan(1, True, True)]
PLAN_LAST = slot_plan(1, True, False)
N0 = len(PROLOGUE)
NG = len(PLAN[0]) + len(PLAN[1])
assert N0 % 2 == 0 and NG % 2 == 0 and UNITS % NP == 0 and UNITS % NH == 0 and UNITS % NDA == 0


def static(g, value):
    return isinstance(g, int) and g == value


def slot_at(g, h, kind, arg):
    if static(g, 0) and h == 0:
        return 2 + PLAN_FIRST.index((kind, arg))
    if static(g, GROUPS - 1) and h == 1:
        return len(PLAN[0]) + PLAN_LAST.index((kind, arg))
    return (len(PLAN[0]) if h else 0) + PLAN[h].index((kind, arg))


def slot_no(g, h, kind, arg):
    return g * NG + (N0 - 2 + slot_at(g, h, kind, arg))


def slot_side(g, h, kind, arg):
    return slot_at(g, h, kind, arg) % 2


TAIL = slot_no(GROUPS - 1, 1, "S", UNITS - 1) + 1


def setup_stage(nc, d, s):
    with ExitStack() as ctx:
        sb = lambda name, shape, dt: ctx.enter_context(nc.sbuf_tensor(name, shape, dt))
        pb = lambda name, shape, dt: ctx.enter_context(nc.psum_tensor(name, shape, dt))
        sem = lambda name: ctx.enter_context(nc.semaphore(name))
        ids = sb("ids", [P, BATCH], I32)
        idf = sb("idf", [P, 3, BATCH], FP32)
        araw = sb("araw", [P, KT, STATE], FP32)
        drow = sb("drow", [RANK, DIM], FP32)
        usum = sb("usum", [RANK, 2], FP32)
        xpw = sb("xpw", [P, KT, XP], FP32)
        dtw = sb("dtw", [DTR, DIM], FP32)
        uct = sb("uct", [P, KT, RANK], FP32)
        mdt = sb("mdt", [DTR, RANK], FP32)
        w16 = sb("w16", [RANK, W_COLS], FP32)
        rest = sb("rest", [RANK, W_COLS], FP32)
        part = sb("part", [RANK, 3, W_COLS], BF16)
        p_ut = pb("p_ut", [P, 512], FP32)
        p_g = pb("p_g", [P, 512], FP32)
        p_bc = pb("p_bc", [P, 512], FP32)
        p_m = pb("p_mt", [P, 512], FP32)
        p_z = pb("p_z", [P, DIM], FP32)

        ids_in, u_in, a_in, w_in, d_in = (sem(n) for n in ("ids_in", "u_in", "a_in", "w_in", "d_in"))
        ident_ok, zero_ok, uc_ok, uct_done, uct_ok = (sem(n) for n in ("ident_ok", "zero_ok", "uc_ok", "uct_done", "uct_ok"))
        m_done, m_ok, z_done, part_ok, stacked = (sem(n) for n in ("m_done", "m_ok", "z_done", "part_ok", "stacked"))
        a_exp, dve_chain = sem("a_exp"), sem("dve_chain")
        block = ctx.enter_context(nc.Block())

        @block.sync
        def _(sp):
            sp.dma_start(w16[:, W_H:W_H + DIM], d["lora_up"]).then_inc(u_in, 16)
            sp.dma_start(xpw[:, :, :], d["xp_wT"].rearrange("(k p) n -> p k n", p=P)).then_inc(w_in, 16)
            sp.dma_start(dtw[:, :], d["dt_wT"]).then_inc(w_in, 16)
            sp.dma_start(drow[:, :], d["D"].to_broadcast([RANK, DIM])).then_inc(d_in, 16)
            sp.dma_start(s["dtb"][:, :], d["dt_b"]).then_inc(d_in, 16)
            for i in range(3):
                sp.wait_ge(part_ok, i + 1)
                for c, which in enumerate(WEIGHT_PARTS):
                    if which == i:
                        sp.dma_start(s["wst"][c * RANK:(c + 1) * RANK, :], part[:, i, :]).then_inc(stacked, 16)
            sp.wait_ge(stacked, 16 * len(WEIGHT_PARTS))
            sp.wait_ge(d_in, 32)

        @block.gpsimd
        def _(pool):
            nc.gpsimd.memset(s["ident"][:, :], 0.0).then_inc(zero_ok, 1)
            pool.wait_ge(zero_ok, 1)
            nc.gpsimd.affine_select(out=s["ident"][:, :], in_=s["ident"][:, :], compare_op=ALU.not_equal, fill=1.0,
                                    base=0, pattern=[[-1, P]], channel_multiplier=1).then_inc(ident_ok, 1)

        @block.scalar
        def _(act):
            act.dma_start(ids[:, :], d["x"]).then_inc(ids_in, 16)
            act.dma_start(araw[:, :, :], d["A_log"].rearrange("(k p) n -> p k n", p=P)).then_inc(a_in, 16)
            act.wait_ge(a_in, 16)
            nc.scalar.activation(s["aneg"][:, :, :], araw[:, :, :], ACT.Exp).then_inc(a_exp, 1)

        @block.tensor
        def _(pe):
            pe.wait_ge(ident_ok, 1)
            pe.wait_ge(uc_ok, 1)
            for k in range(KT):
                last = nc.tensor.transpose(p_ut[:, k * RANK:(k + 1) * RANK], w16[:, W_X + k * P:W_X + (k + 1) * P],
                                           s["ident"][0:RANK, 0:RANK])
            last.then_inc(uct_done, 1)
            pe.wait_ge(uct_ok, 1)
            pe.wait_ge(w_in, 32)
            for k in range(KT):
                nc.tensor.matmul(p_g[0:RANK, 0:RANK], uct[:, k, :], uct[:, k, :], start=k == 0, stop=k == KT - 1)
            for k in range(KT):
                nc.tensor.matmul(p_bc[0:RANK, 0:2 * STATE], uct[:, k, :], xpw[:, k, DTR:XP], start=k == 0, stop=k == KT - 1)
            for k in range(KT):
                last = nc.tensor.matmul(p_m[0:DTR, 0:RANK], xpw[:, k, 0:DTR], uct[:, k, :], start=k == 0, stop=k == KT - 1)
            last.then_inc(m_done, 1)
            pe.wait_ge(m_ok, 1)
            for j in range(2):
                last = nc.tensor.matmul(p_z[0:RANK, j * 512:(j + 1) * 512], mdt[:, :], dtw[:, j * 512:(j + 1) * 512],
                                        start=True, stop=True)
            last.then_inc(z_done, 1)

        @block.vector
        def _(dve):
            chain = [0]

            def link(ins):
                chain[0] += 1
                ins.then_inc(dve_chain, 1)
                dve.wait_ge(dve_chain, chain[0])

            dve.wait_ge(u_in, 16)
            link(nc.vector.reduce_sum(usum[:, 0:1], w16[:, W_H:W_H + DIM], axis=AX.X))
            link(nc.vector.tensor_scalar(usum[:, 1:2], usum[:, 0:1], -1.0 / DIM, None, ALU.mult))
            nc.vector.tensor_scalar(w16[:, W_X:W_X + DIM], w16[:, W_H:W_H + DIM], usum[:, 1:2], None, ALU.add).then_inc(uc_ok, 1)
            dve.wait_ge(uct_done, 1)
            nc.vector.tensor_copy(uct[:, :, :], p_ut[:, 0:KT * RANK].rearrange("p (k n) -> p k n", k=KT)).then_inc(uct_ok, 1)
            dve.wait_ge(ids_in, 16)
            link(nc.vector.tensor_copy(idf[:, 0, :], ids[:, :]))
            link(nc.vector.tensor_scalar(idf[:, 1, :], idf[:, 0, :], 0.0, float(VOCAB), ALU.is_lt, ALU.mult))
            link(nc.vector.tensor_tensor(idf[:, 2, :], idf[:, 0, :], idf[:, 1, :], ALU.add))
            nc.vector.tensor_scalar(s["idx"][:, :], idf[:, 2, :], 0.0, float(VOCAB - 1), ALU.max, ALU.min)
            dve.wait_ge(a_exp, 1)
            nc.vector.tensor_scalar(s["aneg"][:, :, :], s["aneg"][:, :, :], -1.0, None, ALU.mult)
            dve.wait_ge(d_in, 32)
            nc.vector.tensor_tensor(w16[:, W_D:W_D + DIM], w16[:, W_X:W_X + DIM], drow[:, :], ALU.mult)
            dve.wait_ge(m_done, 1)
            nc.vector.tensor_copy(mdt[:, :], p_m[0:DTR, 0:RANK]).then_inc(m_ok, 1)
            nc.vector.tensor_scalar(w16[:, W_G:W_G + RANK], p_g[0:RANK, 0:RANK], 1.0 / DIM, None, ALU.mult)
            nc.vector.tensor_copy(w16[:, W_BC:W_COLS], p_bc[0:RANK, 0:2 * STATE])
            dve.wait_ge(z_done, 1)
            link(nc.vector.tensor_copy(w16[:, W_Z:W_Z + DIM], p_z[0:RANK, :]))
            nc.vector.tensor_copy(part[:, 0, :], w16[:, :]).then_inc(part_ok, 1)
            dve.wait_ge(part_ok, 1)
            link(nc.vector.tensor_tensor(rest[:, :], w16[:, :], part[:, 0, :], ALU.subtract))
            nc.vector.tensor_copy(part[:, 1, :], rest[:, :]).then_inc(part_ok, 1)
            dve.wait_ge(part_ok, 2)
            nc.vector.tensor_tensor(part[:, 2, :], rest[:, :], part[:, 1, :], ALU.subtract).then_inc(part_ok, 1)


def scan_stage(nc, d, s):
    with ExitStack() as ctx:
        sb = lambda name, shape, dt: ctx.enter_context(nc.sbuf_tensor(name, shape, dt))
        pb = lambda name, shape, dt: ctx.enter_context(nc.psum_tensor(name, shape, dt))
        sem = lambda name: ctx.enter_context(nc.semaphore(name))
        eraw = sb("eraw", [P, GB, RANK], FP32)
        esc = sb("esc", [P, GB, RANK], FP32)
        erest = sb("erest", [P, GB, RANK], FP32)
        est = sb("est", [P, 2, GB, STACK], BF16)
        et = sb("et", [STACK, 2, GT], BF16)
        eg = sb("eg", [P, GB, RANK], FP32)
        vsum = sb("vsum", [P, GB], FP32)
        var = sb("var", [P, 5, GB], FP32)
        mhalf = sb("mhalf", [P, GB], FP32)
        c15 = sb("c15", [P, GB], FP32)
        one = sb("one", [P, 1], FP32)
        idcur = sb("idcur", [P, GB], U32)
        ct = sb("ct", [STATE, GT], FP32)
        identb = sb("identb1", [P, P], BF16)
        wabs = sb("wabs", [P, 8], FP32)
        wexp = sb("wexp", [P, DIM], FP32)
        wrow = sb("wrow", [1, P], FP32)
        ones = sb("ones1", [1, P], FP32)
        bnext = sb("bnext", [P, GB, STATE], FP32)
        bcur = sb("bcur", [P, GB, STATE], FP32)
        cbc = sb("cbc", [P, STATE, GT], FP32)
        zb = sb("zb", [P, 2, GT], FP32)
        ez = sb("ez", [P, 2, GT], FP32)
        m30 = sb("m30", [P, 1], FP32)
        ux = sb("ux", [P, 2, GT], FP32)
        dtt = sb("dtt", [P, 2, HT, GT], FP32)
        ut = sb("u_tok", [P, 2, GB, HD], FP32)
        v = sb("v", [P, 2, GB, HD], FP32)
        da = sb("da", [P, NDA, 2, GT], FP32)
        hs = sb("hs", [P, NH, 2 * GT], FP32)
        ps = sb("ps", [P, NP, 2, GT], FP32)
        h2t = sb("h2t", [P, HT, GT], FP32)
        h2o = sb("h2o", [P, 2, 2, HD], FP32)
        slot = pb("slot", [P, 2, 2 * GT], FP32)
        yp = pb("yp", [P, HT, GT], FP32)

        names = ("da_ready v_ready slot_full slot_read p_ready r_done y_read est_ready gathered z_ready e_ready "
                 "sp_ready dt_ready var_ready bcur_ready h2_stored c_stored h2o_ready zero_ok").split()
        (da_ready, v_ready, slot_full, slot_read, p_ready, r_done, y_read, est_ready, gathered, z_ready, e_ready,
         sp_ready, dt_ready, var_ready, bcur_ready, h2_stored0, c_stored, h2o_ready, zero_ok) = (sem(n) for n in names)
        pool_chain, dve_chain, eg_ok, mhalf_ok, w_in, wmax_col, wmax_row, wmax_one, wmax_bc, ones_ok, wq_ok = (
            sem(n) for n in ("pool_chain", "dve_chain1", "eg_ok", "mhalf_ok", "w_in1", "wmax_col", "wmax_row",
                             "wmax_one", "wmax_bc", "ones_ok1", "wq_ok"))
        h2_stored = [h2_stored0, sem("h2_stored1")]
        m30_ok = sem("m30_ok")
        c_loaded = [sem(f"c_loaded{c}") for c in range(4)]
        block = ctx.enter_context(nc.Block())
        h2v = d["h2"].rearrange("(b p) c -> p b c", p=P)
        ident, wst = s["ident"], s["wst"]
        CHAIN = 14
        wraw = [ring[:, :, :, :].rearrange("p a b c -> p (a b c)").rearrange("p (k n) -> p k n", n=DIM)
                for ring in (v, ps)]

        def prep_slot(g, h, kind, arg):
            if isinstance(g, int) and g < 0:
                return PROLOGUE.index((kind, arg)), PROLOGUE.index((kind, arg)) % 2
            return slot_no(g, h, kind, arg), slot_side(g, h, kind, arg)

        def jobs(h, u, last):
            got = PREP_AT[h].get(u, [])
            return [] if last and h == 1 else got

        def z_no(g, h, q):
            return q if isinstance(g, int) and g < 0 else g * 4 + (2 + 2 * h + q)

        def unit_no(g, h, u):
            return g * (2 * UNITS) + (h * UNITS + u)

        def back(g, h, u, n):
            u -= n
            if u < 0:
                u += UNITS
                g, h = (g - 1, 1) if h == 0 else (g, 0)
            if isinstance(g, int) and g < 0:
                return None
            return g, h, u

        def groups(engine, body):
            body(0, False)
            with engine.Fori(1, GROUPS - 1) as g:
                body(g, False)
            body(GROUPS - 1, True)

        @block.sync
        def _(sp):
            def c_job(g, ahead):
                no, _ = prep_slot(g, 1, "C", 0)
                sp.wait_ge(slot_read, no + 1)
                sp.dma_start(d["c"][bass.ds(ahead, 1), :, :].rearrange("o n t -> (o n) t"),
                             ct[:, :]).then_inc(c_stored, 16)
                sp.wait_ge(c_stored, ahead * 16 + 16)
                for c in range(4):
                    if not (isinstance(g, int) and g < 0):
                        sp.wait_ge(p_ready, unit_no(g, 1, 8 * c + 7) + 1)
                    sp.dma_start(cbc[:, 4 * c:4 * c + 4, :],
                                 d["c"][bass.ds(ahead, 1), 4 * c:4 * c + 4, :].rearrange("o n t -> o (n t)")
                                 .to_broadcast([P, 4 * GT])).then_inc(c_loaded[c], 16)

            def h2_job(g, h, gp, hp):
                for bp in range(2):
                    fno = (gp * 2 + hp) * 2 + bp
                    sp.wait_ge(h2o_ready, fno * 2 + 2)
                    sp.dma_start(h2v[:, bass.ds(gp * GB + 2 * bp, 2), hp * HD:(hp + 1) * HD],
                                 h2o[:, bp, :, :]).then_inc(h2_stored[bp], 16)

            def body(g, last):
                if not (isinstance(g, int) and g == 0):
                    h2_job(g, 0, g - 1, 1)
                h2_job(g, 1, g, 0)
                if not last:
                    c_job(g, g + 1)

            wv = d["ffn_wT"].rearrange("(a k p) n -> a p k n", p=P, a=2)
            for i in range(2):
                sp.dma_start(wraw[i], wv[i]).then_inc(w_in, 16)
            c_job(-1, 0)
            groups(nc.sync, body)
            h2_job(GROUPS, 0, GROUPS - 1, 1)
            for bp in range(2):
                sp.wait_ge(h2_stored[bp], 16 * 2 * GROUPS)

        @block.gpsimd
        def _(pool):
            def ids_job(ahead):
                nc.gpsimd.tensor_copy(idcur[:, :], s["idx"][:, bass.ds(ahead * GB, GB)]).then_inc(pool_chain, 1)

            def gather_job():
                for b in range(GB):
                    nc.gpsimd.indirect_dma_start(
                        out=eraw[:, b, :], out_offset=None, in_=d["lora_down"],
                        in_offset=bass.IndirectOffsetOnAxis(ap=idcur[:, b:b + 1], axis=0)).then_inc(gathered, 16)

            def split(src, i, ahead, c):
                at = ahead * CHAIN + c
                view = est[:, i, :, :].rearrange("p b (a r) -> p b a r", r=RANK)
                times = lambda x, n: x.unsqueeze(2).to_broadcast([P, GB, n, RANK])
                unit = lambda n: one[:, :].unsqueeze(2).unsqueeze(3).to_broadcast([P, GB, n, RANK])
                nc.gpsimd.tensor_tensor(view[:, :, 0:3, :], times(src, 3), unit(3), ALU.mult).then_inc(pool_chain, 1)
                pool.wait_ge(pool_chain, at + 1)
                nc.gpsimd.tensor_tensor(erest[:, :, :], src, view[:, :, 0, :], ALU.subtract).then_inc(pool_chain, 1)
                pool.wait_ge(pool_chain, at + 2)
                nc.gpsimd.tensor_tensor(view[:, :, 3:5, :], times(erest[:, :, :], 2), unit(2), ALU.mult).then_inc(pool_chain, 1)
                pool.wait_ge(pool_chain, at + 3)
                nc.gpsimd.tensor_tensor(view[:, :, 5, :], erest[:, :, :], view[:, :, 3, :], ALU.subtract).then_inc(est_ready, 1)
                pool.wait_ge(est_ready, ahead * 2 + (i + 1))

            def split_job(ahead):
                pool.wait_ge(gathered, ahead * (16 * GB) + 16 * GB)
                split(eraw[:, :, :], 0, ahead, 1)

            def rstd_job(ahead):
                at = ahead * CHAIN + 4
                pool.wait_ge(var_ready, ahead + 1)
                nc.gpsimd.tensor_tensor(var[:, 1, :], var[:, 0, :], mhalf[:, :], ALU.pow).then_inc(pool_chain, 1)
                pool.wait_ge(pool_chain, at + 1)
                nc.gpsimd.tensor_tensor(var[:, 2, :], var[:, 1, :], var[:, 1, :], ALU.mult).then_inc(pool_chain, 1)
                pool.wait_ge(pool_chain, at + 2)
                nc.gpsimd.tensor_tensor(var[:, 3, :], var[:, 2, :], var[:, 0, :], ALU.mult).then_inc(pool_chain, 1)
                pool.wait_ge(pool_chain, at + 3)
                nc.gpsimd.tensor_tensor(var[:, 2, :], var[:, 3, :], mhalf[:, :], ALU.mult).then_inc(pool_chain, 1)
                pool.wait_ge(pool_chain, at + 4)
                nc.gpsimd.tensor_tensor(var[:, 3, :], var[:, 2, :], c15[:, :], ALU.add).then_inc(pool_chain, 1)
                pool.wait_ge(pool_chain, at + 5)
                nc.gpsimd.tensor_tensor(var[:, 4, :], var[:, 3, :], var[:, 1, :], ALU.mult).then_inc(pool_chain, 1)
                pool.wait_ge(pool_chain, at + 6)
                nc.gpsimd.tensor_tensor(esc[:, :, :], eraw[:, :, :], var[:, 4, :].unsqueeze(2).to_broadcast([P, GB, RANK]),
                                        ALU.mult).then_inc(pool_chain, 1)
                pool.wait_ge(pool_chain, at + 7)
                split(esc[:, :, :], 1, ahead, 11)

            def dt_job(g, h, q, hn):
                z = z_no(g, h, q)
                pool.wait_ge(sp_ready, z + 1)
                nc.gpsimd.tensor_tensor(dtt[:, hn, 2 * q:2 * q + 2, :], zb[:, :, :], ez[:, :, :], ALU.add).then_inc(dt_ready, 1)

            def cmul(g, h, u):
                n, q = u // 2, u % 2
                sno = slot_no(g, h, "S", u)
                if n % 4 == 0 and q == 0 and h == 0:
                    pool.wait_ge(c_loaded[n // 4], g * 16 + 16)
                pool.wait_ge(slot_read, sno + 1)
                b = back(g, h, u, NP)
                if b:
                    pool.wait_ge(r_done, unit_no(*b) + 1)
                nc.gpsimd.tensor_tensor(ps[:, u % NP, :, :], hs[:, u % NH, :].rearrange("p (j t) -> p j t", j=2),
                                        cbc[:, n:n + 1, :].to_broadcast([P, 2, GT]), ALU.mult).then_inc(p_ready, 1)

            def body(g, last):
                for h in range(2):
                    for u in range(UNITS):
                        if h == 1 and u == GATHER_AT and not last:
                            pool.wait_ge(pool_chain, g * CHAIN + (CHAIN + 1))
                        cmul(g, h, u)
                        if last and h == 1:
                            continue
                        if h == 1 and u == GATHER_AT - 1:
                            ids_job(g + 1)
                        if h == 1 and u == GATHER_AT:
                            gather_job()
                        if h == 1 and u == SPLIT_AT:
                            split_job(g + 1)
                        if h == 1 and u == RSTD_AT:
                            rstd_job(g + 1)
                        for q in range(2):
                            if u == Z_AT[h][q] + DT_AFTER:
                                dt_job(g, h, q, 1 - h)

            nc.gpsimd.memset(mhalf[:, :], -0.5)
            nc.gpsimd.memset(one[:, :], 1.0)
            nc.gpsimd.memset(c15[:, :], 1.5).then_inc(mhalf_ok, 1)
            ids_job(0)
            pool.wait_ge(pool_chain, 1)
            gather_job()
            pool.wait_ge(mhalf_ok, 1)
            split_job(0)
            rstd_job(0)
            for q in range(2):
                dt_job(-1, 1, q, 0)
            pool.wait_ge(wq_ok, KT)
            groups(nc.gpsimd, body)

        @block.scalar
        def _(act):
            def softplus_job(g, h, q):
                z = z_no(g, h, q)
                act.wait_ge(z_ready, z + 1)
                nc.scalar.activation(ez[:, :, :], ez[:, :, :], ACT.Exp).then_inc(e_ready, 1)
                nc.scalar.activation(zb[:, :, :], zb[:, :, :], ACT.Relu, bias=m30[:, :])
                act.wait_ge(e_ready, z + 1)
                nc.scalar.activation(ez[:, :, :], ez[:, :, :], ACT.Ln, bias=1.0).then_inc(sp_ready, 1)

            def b_mul(g, h, n):
                b = back(g, h, 2 * n, 4)
                if b:
                    act.wait_ge(slot_full, slot_no(b[0], b[1], "S", b[2] + 1) + 1)
                for i in range(GB):
                    m = nc.scalar.activation(v[:, n % 2, i, :], ut[:, h, i, :], ACT.Copy, scale=bcur[:, i, n:n + 1])
                m.then_inc(v_ready, 1)

            def exp_a(g, h, u):
                n, q = u // 2, u % 2
                b = back(g, h, u, NDA)
                if b:
                    act.wait_ge(slot_read, slot_no(b[0], b[1], "S", b[2]) + 1)
                for j in range(2):
                    t = 2 * q + j
                    m = nc.scalar.activation(
                        da[:, u % NDA, j, :].rearrange("p (b t) -> p b t", b=GB)[:, :, 1:SEQ],
                        dtt[:, h, t, :].rearrange("p (b t) -> p b t", b=GB)[:, :, 1:SEQ],
                        ACT.Exp, scale=s["aneg"][:, h * HT + t, n:n + 1])
                m.then_inc(da_ready, 1)

            def body(g, last):
                for h in range(2):
                    if h == 0:
                        no = slot_no(g - 1, 1, "C", 0) if not isinstance(g, int) or g > 0 else PROLOGUE.index(("C", 0))
                        act.wait_ge(slot_read, no + 1)
                        if not static(g, 0):
                            act.wait_ge(v_ready, g * (2 * STATE))
                        nc.scalar.activation(bcur[:, :, :], bnext[:, :, :], ACT.Copy).then_inc(bcur_ready, 1)
                        act.wait_ge(bcur_ready, g + 1)
                    if h == 1:
                        no = slot_no(g, 0, "U", 1)
                    else:
                        no = slot_no(g - 1, 1, "U", 1) if not isinstance(g, int) or g > 0 else PROLOGUE.index(("U", 1))
                    act.wait_ge(slot_read, no + 1)
                    for u in range(UNITS):
                        if u % 2 == 0:
                            b_mul(g, h, u // 2)
                        exp_a(g, h, u)
                        if last and h == 1:
                            continue
                        for q in range(2):
                            if u == Z_AT[h][q] + ACT_AFTER:
                                softplus_job(g, h, q)

            nc.scalar.preload_act_table_set("natural_log_exp_and_others")
            act.wait_ge(m30_ok, 1)
            for q in range(2):
                softplus_job(-1, 1, q)
            act.wait_ge(zero_ok, 1)
            act.wait_ge(wq_ok, KT)
            groups(nc.scalar, body)

        @block.tensor
        def _(pe):
            def free_slot(no):
                if isinstance(no, int) and no < 2:
                    return
                pe.wait_ge(slot_read, no - 1)

            def trans(g, h, u):
                n, q = u // 2, u % 2
                no, side = slot_no(g, h, "S", u), slot_side(g, h, "S", u)
                free_slot(no)
                if q == 0:
                    pe.wait_ge(v_ready, g * (2 * STATE) + (h * STATE + n + 1))
                for j in range(2):
                    for b in range(GB):
                        m = nc.tensor.transpose(slot[:, side, j * GT + b * P:j * GT + (b + 1) * P],
                                                v[:, n % 2, b, (2 * q + j) * P:(2 * q + j + 1) * P], ident[:, :])
                m.then_inc(slot_full, 1)

            def reduce_n(g, h, u):
                n, q = u // 2, u % 2
                pe.wait_ge(p_ready, unit_no(g, h, u) + 1)
                for j in range(2):
                    m = nc.tensor.matmul(yp[:, 2 * q + j, :], ident[:, :], ps[:, u % NP, j, :],
                                         start=False, stop=n == STATE - 1)
                m.then_inc(r_done, 1)

            def residual(g, h, q):
                if not (isinstance(g, int) and g == 0 and h == 0):
                    pe.wait_ge(y_read, g * 4 + (2 * h + q - 1))
                for j in range(2):
                    c = (h * HT + 2 * q + j) * P
                    nc.tensor.matmul(yp[:, 2 * q + j, :], wst[:, W_H + c:W_H + c + P], et[:, 0, :], start=True, stop=False)
                    nc.tensor.matmul(yp[:, 2 * q + j, :], wst[:, W_D + c:W_D + c + P], et[:, 1, :], start=False, stop=False)

            def h2_trans(no, side, bp, yno):
                free_slot(no)
                pe.wait_ge(y_read, yno)
                for b in range(2):
                    for t in range(HT):
                        m = nc.tensor.transpose(slot[:, side, b * HD + t * P:b * HD + (t + 1) * P],
                                                h2t[:, t, (2 * bp + b) * P:(2 * bp + b + 1) * P], ident[:, :])
                m.then_inc(slot_full, 1)

            def prep(g, h, kind, arg, ahead):
                no, side = prep_slot(g, h, kind, arg)
                free_slot(no)
                if kind in "ER":
                    i = int(kind == "R")
                    pe.wait_ge(est_ready, ahead * 2 + (i + 1))
                    half = slot[:, side, :].bitcast(BF16)
                    for b in range(GB):
                        m = nc.tensor.transpose(half[0:STACK, b * P:(b + 1) * P], est[:, i, b, :], identb[:, :])
                if kind == "G":
                    pe.wait_ge(slot_read, prep_slot(g, h, "E", 0)[0] + 1)
                    for b in range(GB):
                        m = nc.tensor.matmul(slot[:, side, b * RANK:(b + 1) * RANK], et[:, 0, b * P:(b + 1) * P],
                                             wst[:, W_G:W_G + RANK], start=True, stop=True)
                if kind == "C":
                    pe.wait_ge(slot_read, prep_slot(g, h, "R", 0)[0] + 1)
                    nc.tensor.matmul(slot[0:STATE, side, 0:GT], wst[:, W_BC + STATE:W_COLS], et[:, 1, :], start=True, stop=True)
                    for b in range(GB):
                        m = nc.tensor.matmul(slot[:, side, GT + b * STATE:GT + (b + 1) * STATE], et[:, 1, b * P:(b + 1) * P],
                                             wst[:, W_BC:W_BC + STATE], start=True, stop=True)
                if kind in "ZX":
                    for j in range(2):
                        c = (W_Z if kind == "Z" else W_X) + ((1 - h) * HT + 2 * arg + j) * P
                        m = nc.tensor.matmul(slot[:, side, j * GT:(j + 1) * GT], wst[:, c:c + P], et[:, 1, :],
                                             start=True, stop=True)
                if kind == "U":
                    pe.wait_ge(slot_read, prep_slot(g, h, "X", arg)[0] + 1)
                    for b in range(GB):
                        for j in range(2):
                            m = nc.tensor.transpose(slot[:, side, (b * 2 + j) * P:(b * 2 + j + 1) * P],
                                                    ux[:, j, b * P:(b + 1) * P], ident[:, :])
                m.then_inc(slot_full, 1)

            def body(g, last):
                for h in range(2):
                    first = isinstance(g, int) and g == 0 and h == 0
                    for u in range(UNITS):
                        trans(g, h, u)
                        if u in (LAG, LAG + 1):
                            residual(g, h, u - LAG)
                        b = back(g, h, u, LAG)
                        if b:
                            reduce_n(*b)
                        if u == F_AT and not first:
                            for bp in range(2):
                                h2_trans(slot_no(g, h, "F", bp), slot_side(g, h, "F", bp), bp, g * 4 + 2 * h)
                        for kind, arg in jobs(h, u, last):
                            prep(g, h, kind, arg, g + 1)

            pe.wait_ge(ones_ok, 1)
            pe.wait_ge(wmax_col, 1)
            nc.tensor.transpose(yp[0:1, 0, 0:P], wabs[:, 2:3], ident[:, :]).then_inc(wmax_row, 1)
            pe.wait_ge(wmax_one, 1)
            nc.tensor.matmul(yp[:, 1, 0:1], ones[0:1, :], wrow[0:1, 0:1], start=True, stop=True).then_inc(wmax_bc, 1)
            for kind, arg in PROLOGUE:
                prep(-1, 1, kind, arg, 0)
            groups(nc.tensor, body)
            for u in range(UNITS - LAG, UNITS):
                reduce_n(GROUPS - 1, 1, u)
            for bp in range(2):
                no, side = TAIL + bp, bp
                h2_trans(no, side, bp, 4 * GROUPS)

        @block.vector
        def _(dve):
            def scan(g, h, u):
                no, side = slot_no(g, h, "S", u), slot_side(g, h, "S", u)
                dve.wait_ge(da_ready, unit_no(g, h, u) + 1)
                dve.wait_ge(slot_full, no + 1)
                b = back(g, h, u, NH)
                if b:
                    dve.wait_ge(p_ready, unit_no(*b) + 1)
                nc.vector.tensor_tensor_scan(hs[:, u % NH, :], da[:, u % NDA, :, :].rearrange("p j t -> p (j t)"),
                                             slot[:, side, :], 0.0, ALU.mult, ALU.add).then_inc(slot_read, 1)

            def y_out(g, h, q):
                dve.wait_ge(r_done, unit_no(g, h, UNITS - 2 + q) + 1)
                nc.vector.tensor_copy(h2t[:, 2 * q:2 * q + 2, :], yp[:, 2 * q:2 * q + 2, :]).then_inc(y_read, 1)

            def h2_out(no, side, bp, g, h):
                dve.wait_ge(slot_full, no + 1)
                blk = g * 2 + h
                if not (isinstance(blk, int) and blk == 0):
                    dve.wait_ge(h2_stored[bp], blk * 16)
                tile = g * GB + 2 * bp
                for b in range(2):
                    part = slot[:, side, b * HD:(b + 1) * HD]
                    nc.vector.bn_stats(s["stats"][:, bass.ds(tile + b, 1), h, :].rearrange("p o f -> p (o f)"), part)
                    nc.vector.tensor_scalar(h2o[:, bp, b, :], part, 1.0, None, ALU.mult, ALU.max,
                                            accum_out=s["hmax"][:, bass.ds(tile + b, 1), h]).then_inc(h2o_ready, 1)
                nc.vector.tensor_reduce(s["hmin"][:, bass.ds(tile, 2), h],
                                        slot[:, side, :].rearrange("p (b c) -> p b c", b=2), AX.X, ALU.min).then_inc(slot_read, 1)

            def prep(g, h, kind, arg, ahead):
                no, side = prep_slot(g, h, kind, arg)
                dve.wait_ge(slot_full, no + 1)
                if kind in "ER":
                    m = nc.vector.tensor_copy(et[:, int(kind == "R"), :], slot[:, side, :].bitcast(BF16)[0:STACK, 0:GT])
                if kind == "G":
                    nc.vector.tensor_tensor(eg[:, :, :], slot[:, side, 0:GB * RANK].rearrange("p (b n) -> p b n", b=GB),
                                            eraw[:, :, :], ALU.mult).then_inc(slot_read, 1)
                    dve.wait_ge(slot_read, no + 1)
                    nc.vector.reduce_sum(vsum[:, :], eg[:, :, :], axis=AX.X).then_inc(eg_ok, 1)
                    dve.wait_ge(eg_ok, ahead + 1)
                    nc.vector.tensor_scalar(var[:, 0, :], vsum[:, :], 0.0, EPS, ALU.max, ALU.add).then_inc(var_ready, 1)
                    return
                if kind == "C":
                    if not static(g, -1):
                        dve.wait_ge(c_stored, ahead * 16)
                        dve.wait_ge(bcur_ready, ahead)
                    nc.vector.tensor_copy(bnext[:, :, :], slot[:, side, GT:GT + GB * STATE].rearrange("p (b n) -> p b n", b=GB))
                    m = nc.vector.tensor_copy(ct[:, :], slot[0:STATE, side, 0:GT])
                if kind == "Z":
                    z = z_no(g, h, arg)
                    if not (isinstance(z, int) and z == 0):
                        dve.wait_ge(dt_ready, z)
                    for j in range(2):
                        k = (1 - h) * HT + 2 * arg + j
                        m = nc.vector.tensor_scalar(zb[:, j, :], slot[:, side, j * GT:(j + 1) * GT],
                                                    s["dtb"][:, k:k + 1], None, ALU.add)
                    m.then_inc(slot_read, 1)
                    dve.wait_ge(slot_read, no + 1)
                    nc.vector.tensor_scalar(ez[:, :, :], zb[:, :, :], 30.0, None, ALU.min).then_inc(z_ready, 1)
                    return
                if kind == "X":
                    dve.wait_ge(dt_ready, z_no(g, h, arg) + 1)
                    m = nc.vector.tensor_tensor(ux[:, :, :], slot[:, side, :].rearrange("p (j t) -> p j t", j=2),
                                                dtt[:, 1 - h, 2 * arg:2 * arg + 2, :], ALU.mult)
                if kind == "U":
                    m = nc.vector.tensor_copy(ut[:, 1 - h, :, arg * 2 * P:(arg + 1) * 2 * P],
                                              slot[:, side, :].rearrange("p (b c) -> p b c", b=GB))
                m.then_inc(slot_read, 1)

            def body(g, last):
                for h in range(2):
                    first = isinstance(g, int) and g == 0 and h == 0
                    gp, hp = (g - 1, 1) if h == 0 else (g, 0)
                    for u in range(UNITS):
                        scan(g, h, u)
                        if not first and u in (LAG - 2, LAG - 1):
                            y_out(gp, hp, u - (LAG - 2))
                        if u == F_AT and not first:
                            for bp in range(2):
                                h2_out(slot_no(g, h, "F", bp), slot_side(g, h, "F", bp), bp, gp, hp)
                        for kind, arg in jobs(h, u, last):
                            prep(g, h, kind, arg, g + 1)

            nc.vector.tensor_copy(identb[:, :], ident[:, :])
            nc.vector.memset(ones[:, :], 1.0).then_inc(ones_ok, 1)
            nc.vector.memset(m30[:, :], -30.0).then_inc(m30_ok, 1)
            for c in range(NDA):
                z0 = nc.vector.memset(da[:, c, :, :].rearrange("p j (b t) -> p (j b) t", t=SEQ)[:, :, 0:1], 0.0)
            z0.then_inc(zero_ok, 1)
            chain = [0]

            def link(ins):
                chain[0] += 1
                ins.then_inc(dve_chain, 1)
                dve.wait_ge(dve_chain, chain[0])

            dve.wait_ge(w_in, 32)
            for i in range(2):
                link(nc.vector.tensor_reduce(wabs[:, i:i + 1], wraw[i], AX.XY, ALU.max, apply_absolute_value=True))
            nc.vector.tensor_tensor(wabs[:, 2:3], wabs[:, 0:1], wabs[:, 1:2], ALU.max).then_inc(wmax_col, 1)
            dve.wait_ge(wmax_row, 1)
            nc.vector.reduce_max(wrow[0:1, 0:1], yp[0:1, 0, 0:P], axis=AX.X).then_inc(wmax_one, 1)
            dve.wait_ge(wmax_bc, 1)
            link(nc.vector.tensor_scalar(s["winv"][:, :], yp[:, 1, 0:1], 1e-12, 1.0 / FP8_MAX, ALU.max, ALU.mult))
            link(nc.vector.reciprocal(wabs[:, 3:4], s["winv"][:, :]))

            def round_weight(k):
                wk = wraw[k // 4][:, k % 4, :]
                link(nc.vector.tensor_scalar(wk, wk, wabs[:, 3:4], None, ALU.mult))
                link(nc.vector.tensor_scalar(wexp[:, :].bitcast(I32), wk.bitcast(I32), EXP_BITS, None, ALU.bitwise_and))
                link(nc.vector.tensor_scalar(wexp[:, :], wexp[:, :], MIN_NORMAL, ROUND, ALU.max, ALU.mult))
                link(nc.vector.tensor_tensor(wk, wk, wexp[:, :], ALU.add))
                nc.vector.tensor_tensor(s["wq"][:, k, :], wk, wexp[:, :], ALU.subtract).then_inc(wq_ok, 1)
                dve.wait_ge(wq_ok, k + 1)

            for i, (kind, arg) in enumerate(PROLOGUE):
                prep(-1, 1, kind, arg, 0)
                if i < KT:
                    round_weight(i)
            groups(nc.vector, body)
            for q in range(2):
                y_out(GROUPS - 1, 1, q)
            for bp in range(2):
                h2_out(TAIL + bp, bp, bp, GROUPS - 1, 1)


def ffn_stage(nc, d, s):
    with ExitStack() as ctx:
        sb = lambda name, shape, dt: ctx.enter_context(nc.sbuf_tensor(name, shape, dt))
        pb = lambda name, shape, dt: ctx.enter_context(nc.psum_tensor(name, shape, dt))
        sem = lambda name: ctx.enter_context(nc.semaphore(name))
        UN = 4
        TURNS = BATCH // UN
        ms = sb("ms", [P, 4, BATCH], FP32)
        dev = sb("dev", [P, BATCH, 4], FP32)
        mean = sb("mean", [P, BATCH], FP32)
        std = sb("std", [P, BATCH], FP32)
        rstd = sb("rstd", [P, BATCH], FP32)
        ext = sb("ext", [P, 2, BATCH], FP32)
        sc = sb("sc", [P, BATCH], FP32)
        nb = sb("nb", [P, BATCH], FP32)
        cm = sb("cm", [P, 4], FP32)
        row = sb("row2", [1, P], FP32)
        ones = sb("ones2", [1, P], FP32)
        identb = sb("identb", [P, P], BF16)
        wq = s["wq"]
        bias = sb("bias", [P, DIM], FP32)
        h2 = sb("h2_in", [P, UN, DIM], FP32)
        hb = sb("hb", [P, 2, DIM], FP32)
        v = sb("v2", [P, 2, DIM], FP32)
        e = sb("e2", [P, DIM], FP32)
        m = sb("m2", [P, DIM], FP32)
        w = sb("w2", [P, DIM], FP32)
        q = sb("q2", [P, 2, DIM], BF16)
        qt = sb("qt", [P, 2, KT, P], BF16)
        o = sb("o", [P, 2, DIM], FP32)
        p_m = pb("p_m", [P, 512], FP32)
        qp = pb("qp", [P, 2, KT * P], BF16)
        acc = pb("acc", [P, 2, DIM], FP32)
        names = ("identb_ok bias_in var_ok std_ok cm_ok row_done max_ok bc_done ones_ok scale_ok dve_chain h2_used "
                 "v_ready hb_ready q_ready qp_ready qt_ready acc_ready o_ready").split()
        (identb_ok, bias_in, var_ok, std_ok, cm_ok, row_done, max_ok, bc_done, ones_ok, scale_ok, dve_chain, _,
         v_ready, hb_ready, q_ready, qp_ready, qt_ready, acc_ready, o_ready) = (sem("f_" + n) for n in names)
        h2_in = [sem(f"f_h2_in{j}") for j in range(UN)]
        o_out = [sem(f"f_o_out{j}") for j in range(2)]
        block = ctx.enter_context(nc.Block())
        h2v = d["h2"].rearrange("(b p) c -> p b c", p=P)
        ov = d["out"].rearrange("(b p) c -> p b c", p=P)

        def turns(engine, body):
            body(0)
            with engine.Fori(1, TURNS) as i:
                body(i)

        @block.sync
        def _(sp):
            sp.dma_start(bias[:, :], d["ffn_b"].to_broadcast([P, DIM])).then_inc(bias_in, 16)

            def body(i):
                for j in range(UN):
                    if not static(i, 0):
                        sp.wait_ge(v_ready, i * UN + (j - UN + 1))
                        sp.wait_ge(hb_ready, i * UN + (j - UN + 1))
                    sp.dma_start(h2[:, j, :], h2v[:, bass.ds(i * UN + j, 1), :].rearrange("p o c -> p (o c)")).then_inc(h2_in[j], 16)

            turns(nc.sync, body)

        @block.gpsimd
        def _(pool):
            pool.wait_ge(bias_in, 16)

            def body(i):
                for j in range(UN):
                    pool.wait_ge(h2_in[j], i * 16 + 16)
                    if not (static(i, 0) and j < 2):
                        pool.wait_ge(o_ready, i * UN + (j - 1))
                    nc.gpsimd.tensor_tensor(hb[:, j % 2, :], h2[:, j, :], bias[:, :], ALU.add).then_inc(hb_ready, 1)

            turns(nc.gpsimd, body)

        @block.scalar
        def _(act):
            act.wait_ge(var_ok, 1)
            nc.scalar.activation(std[:, :], ms[:, 1, :], ACT.Sqrt).then_inc(std_ok, 1)
            act.wait_ge(scale_ok, 1)

            def store(i, j):
                act.wait_ge(o_ready, i * UN + (j + 1))
                act.dma_start(ov[:, bass.ds(i * UN + j, 1), :].rearrange("p o c -> p (o c)"), o[:, j % 2, :]).then_inc(o_out[j % 2], 16)

            def body(i):
                for j in range(UN):
                    act.wait_ge(h2_in[j], i * 16 + 16)
                    if not (static(i, 0) and j < 2):
                        act.wait_ge(q_ready, i * UN + (j - 1))
                    nc.scalar.activation(v[:, j % 2, :], h2[:, j, :], ACT.Identity, bias=nb[:, bass.ds(i * UN + j, 1)],
                                         scale=sc[:, bass.ds(i * UN + j, 1)]).then_inc(v_ready, 1)
                    if not (static(i, 0) and j == 0):
                        qt_copy(i, j - 1)
                    if not (static(i, 0) and j < 2):
                        store(i, j - 2)

            def qt_copy(i, j):
                act.wait_ge(qp_ready, i * UN + (j + 1))
                if not (static(i, 0) and j < 2):
                    act.wait_ge(acc_ready, i * UN + (j - 1))
                nc.scalar.activation(qt[:, j % 2, :, :], qp[:, j % 2, :].rearrange("p (k t) -> p k t", k=KT),
                                     ACT.Copy).then_inc(qt_ready, 1)

            turns(nc.scalar, body)
            qt_copy(TURNS - 1, UN - 1)
            store(TURNS - 1, UN - 2)
            store(TURNS - 1, UN - 1)
            for j in range(2):
                act.wait_ge(o_out[j], 16 * BATCH // 2)

        @block.tensor
        def _(pe):
            pe.wait_ge(cm_ok, 1)
            nc.tensor.transpose(p_m[0:1, 0:P], cm[:, 0:1], s["ident"][:, :]).then_inc(row_done, 1)
            pe.wait_ge(ones_ok, 1)
            pe.wait_ge(max_ok, 1)
            nc.tensor.matmul(p_m[:, P:P + 1], ones[0:1, :], row[0:1, 0:1], start=True, stop=True).then_inc(bc_done, 1)
            pe.wait_ge(identb_ok, 1)

            def transposes(i, j):
                pe.wait_ge(q_ready, i * UN + (j + 1))
                if not (static(i, 0) and j < 2):
                    pe.wait_ge(qt_ready, i * UN + (j - 1))
                for k in range(KT):
                    t = nc.tensor.transpose(qp[:, j % 2, k * P:(k + 1) * P], q[:, j % 2, k * P:(k + 1) * P], identb[:, :])
                t.then_inc(qp_ready, 1)

            def products(i, j):
                pe.wait_ge(qt_ready, i * UN + (j + 1))
                if not (static(i, 0) and j < 2):
                    pe.wait_ge(o_ready, i * UN + (j - 1))
                for n in range(2):
                    for k in range(KT):
                        t = nc.tensor.matmul(acc[:, j % 2, n * HD:(n + 1) * HD], qt[:, j % 2, k, :],
                                             wq[:, k, n * HD:(n + 1) * HD], start=k == 0, stop=k == KT - 1)
                t.then_inc(acc_ready, 1)

            def body(i):
                for j in range(UN):
                    transposes(i, j)
                    if not (static(i, 0) and j == 0):
                        products(i, j - 1)

            turns(nc.tensor, body)
            products(TURNS - 1, UN - 1)

        @block.vector
        def _(dve):
            chain = [0]

            def link(ins):
                chain[0] += 1
                ins.then_inc(dve_chain, 1)
                dve.wait_ge(dve_chain, chain[0])

            part = s["stats"][:, :, :, :].rearrange("p b h (a c) -> p b (h a) c", c=3)
            link(nc.vector.reduce_sum(ms[:, 0, :], part[:, :, :, 1], axis=AX.X))
            link(nc.vector.tensor_scalar(mean[:, :], ms[:, 0, :], 0.25, None, ALU.mult))
            link(nc.vector.tensor_tensor(dev[:, :, :], part[:, :, :, 1],
                                         mean[:, :].unsqueeze(2).to_broadcast([P, BATCH, 4]), ALU.subtract))
            link(nc.vector.tensor_tensor(dev[:, :, :], dev[:, :, :], dev[:, :, :], ALU.mult))
            link(nc.vector.scalar_tensor_tensor(dev[:, :, :], dev[:, :, :], DIM / 4.0, part[:, :, :, 2], ALU.mult, ALU.add))
            link(nc.vector.reduce_sum(ms[:, 0, :], dev[:, :, :], axis=AX.X))
            nc.vector.tensor_scalar(ms[:, 1, :], ms[:, 0, :], 1.0 / DIM, EPS, ALU.mult, ALU.add).then_inc(var_ok, 1)
            dve.wait_ge(std_ok, 1)
            link(nc.vector.reciprocal(rstd[:, :], std[:, :]))
            link(nc.vector.tensor_tensor(ext[:, 0, :], s["hmax"][:, :, 0], s["hmax"][:, :, 1], ALU.max))
            link(nc.vector.tensor_tensor(ext[:, 1, :], s["hmin"][:, :, 0], s["hmin"][:, :, 1], ALU.min))
            link(nc.vector.tensor_tensor(ext[:, 0, :], ext[:, 0, :], mean[:, :], ALU.subtract))
            link(nc.vector.tensor_tensor(ext[:, 1, :], mean[:, :], ext[:, 1, :], ALU.subtract))
            link(nc.vector.tensor_tensor(ext[:, 0, :], ext[:, 0, :], ext[:, 1, :], ALU.max))
            link(nc.vector.tensor_tensor(ext[:, 0, :], ext[:, 0, :], rstd[:, :], ALU.mult))
            nc.vector.reduce_max(cm[:, 0:1], ext[:, 0, :], axis=AX.X).then_inc(cm_ok, 1)
            nc.vector.memset(ones[:, :], 1.0).then_inc(ones_ok, 1)
            nc.vector.tensor_copy(identb[:, :], s["ident"][:, :]).then_inc(identb_ok, 1)
            dve.wait_ge(row_done, 1)
            nc.vector.reduce_max(row[0:1, 0:1], p_m[0:1, 0:P], axis=AX.X).then_inc(max_ok, 1)
            dve.wait_ge(bc_done, 1)
            link(nc.vector.tensor_scalar(cm[:, 1:2], p_m[:, P:P + 1], 1e-12, 1.0 / FP8_MAX, ALU.max, ALU.mult))
            link(nc.vector.reciprocal(cm[:, 2:3], cm[:, 1:2]))
            link(nc.vector.tensor_tensor(cm[:, 3:4], cm[:, 1:2], s["winv"][:, :], ALU.mult))
            link(nc.vector.tensor_scalar(sc[:, :], rstd[:, :], cm[:, 2:3], None, ALU.mult))
            nc.vector.scalar_tensor_tensor(nb[:, :], mean[:, :], -1.0, sc[:, :], ALU.mult, ALU.mult).then_inc(scale_ok, 1)

            def round_tile(i, j):
                c = i * (3 * UN) + (chain0 + 3 * j)
                dve.wait_ge(v_ready, i * UN + (j + 1))
                nc.vector.tensor_scalar(e[:, :].bitcast(I32), v[:, j % 2, :].bitcast(I32), EXP_BITS, None,
                                        ALU.bitwise_and).then_inc(dve_chain, 1)
                dve.wait_ge(dve_chain, c + 1)
                nc.vector.tensor_scalar(m[:, :], e[:, :], MIN_NORMAL, ROUND, ALU.max, ALU.mult).then_inc(dve_chain, 1)
                dve.wait_ge(dve_chain, c + 2)
                nc.vector.tensor_tensor(w[:, :], v[:, j % 2, :], m[:, :], ALU.add).then_inc(dve_chain, 1)
                dve.wait_ge(dve_chain, c + 3)
                if not (static(i, 0) and j < 2):
                    dve.wait_ge(qp_ready, i * UN + (j - 1))
                nc.vector.tensor_tensor(q[:, j % 2, :], w[:, :], m[:, :], ALU.subtract).then_inc(q_ready, 1)

            def output(i, j):
                dve.wait_ge(acc_ready, i * UN + (j + 1))
                dve.wait_ge(hb_ready, i * UN + (j + 1))
                if static(i, 0) and j < 2:
                    pass
                elif j < 2:
                    dve.wait_ge(o_out[j % 2], i * 32 + 16 * (j // 2))
                else:
                    dve.wait_ge(o_out[j % 2], i * 32 + 16)
                nc.vector.scalar_tensor_tensor(o[:, j % 2, :], acc[:, j % 2, :], cm[:, 3:4], hb[:, j % 2, :],
                                               ALU.mult, ALU.add).then_inc(o_ready, 1)

            def body(i):
                for j in range(UN):
                    round_tile(i, j)
                    if not (static(i, 0) and j < 2):
                        gi, gj = (i, j - 2) if j >= 2 else (i - 1, j + 2)
                        output(gi, gj)

            chain0 = chain[0]
            turns(nc.vector, body)
            output(TURNS - 1, UN - 2)
            output(TURNS - 1, UN - 1)


def build(nc, d):
    d["h2"] = nc.dram_tensor("h2_scratch", (BATCH * SEQ, DIM), FP32, kind="Internal").ap()
    d["c"] = nc.dram_tensor("c_scratch", (GROUPS, STATE, GT), FP32, kind="Internal").ap()
    with ExitStack() as ctx:
        s = {}
        for name, shape, dt in (
                ("ident", [P, P], FP32),
                ("winv", [P, 1], FP32),
                ("stats", [P, BATCH, 2, 6], FP32),
                ("hmax", [P, BATCH, 2], FP32),
                ("hmin", [P, BATCH, 2], FP32),
                ("idx", [P, BATCH], U32),
                ("wst", [STACK, W_COLS], BF16),
                ("wq", [P, KT, DIM], BF16),
                ("dtb", [P, KT], FP32),
                ("aneg", [P, KT, STATE], FP32)):
            s[name] = ctx.enter_context(nc.sbuf_tensor("s_" + name, shape, dt))
        setup_stage(nc, d, s)
        scan_stage(nc, d, s)
        ffn_stage(nc, d, s)


def kernel(x, L0_tok_lora_down, L0_tok_lora_up, L0_attn_A_log, L0_attn_D, L0_attn_x_proj_w, L0_attn_dt_proj_w,
           L0_attn_dt_proj_b, L0_ffn_weight, L0_ffn_bias):
    import numpy as np
    import concourse.bacc as bacc
    from concourse.bass_utils import run_bass_kernel_spmd

    arrays = {
        "x": np.ascontiguousarray(np.asarray(x).T),
        "lora_down": np.ascontiguousarray(L0_tok_lora_down),
        "lora_up": np.ascontiguousarray(L0_tok_lora_up),
        "A_log": np.ascontiguousarray(L0_attn_A_log),
        "D": np.ascontiguousarray(np.asarray(L0_attn_D).reshape(1, DIM)),
        "xp_wT": np.ascontiguousarray(np.asarray(L0_attn_x_proj_w).T),
        "dt_wT": np.ascontiguousarray(np.asarray(L0_attn_dt_proj_w).T),
        "dt_b": np.ascontiguousarray(np.asarray(L0_attn_dt_proj_b).reshape(KT, P).T),
        "ffn_wT": np.ascontiguousarray(np.asarray(L0_ffn_weight).T),
        "ffn_b": np.ascontiguousarray(np.asarray(L0_ffn_bias).reshape(1, DIM)),
    }
    nc = bacc.Bacc("TRN2", target_bir_lowering=False, num_devices=1)
    d, feeds = {}, {}
    for name, a in arrays.items():
        feeds["in_" + name] = a
        d[name] = nc.dram_tensor("in_" + name, a.shape, mybir.dt.from_np(a.dtype), kind="ExternalInput").ap()
    out = nc.dram_tensor("out_h", (BATCH * SEQ, DIM), FP32, kind="ExternalOutput")
    d["out"] = out.ap()
    build(nc, d)
    r = run_bass_kernel_spmd(nc, [feeds], core_ids=[0])
    return r.results[0]["out_h"].reshape(BATCH, SEQ, DIM)
```

```python
import concourse.bass as bass
from concourse import mybir
from contextlib import ExitStack

FP32 = mybir.dt.float32
BF16 = mybir.dt.bfloat16
I32 = mybir.dt.int32
U32 = mybir.dt.uint32
ALU = mybir.AluOpType
ACT = mybir.ActivationFunctionType
AX = mybir.AxisListType

P = 128
BATCH, SEQ = 64, 128
VOCAB, RANK = 8000, 16
DIM = 1024
STATE = 16
DTR = 32
XP = DTR + 2 * STATE
KT = DIM // P
GB = 4
GROUPS = BATCH // GB
GT = GB * SEQ
HT = KT // 2
HD = HT * P
STACK = 6 * RANK
UNITS = STATE * 2
EPS = 1e-5
FP8_MAX = 448.0
EXP_BITS = 0x7F800000
MIN_NORMAL = 2.0 ** -6
ROUND = 1.5 * 2.0 ** 20

WEIGHT_PARTS = (0, 1, 2, 0, 1, 0)
W_X = 0
W_Z = W_X + DIM
W_H = W_Z + DIM
W_D = W_H + DIM
W_G = W_D + DIM
W_BC = W_G + RANK
W_COLS = W_BC + 2 * STATE
FOLD = 8

LAG = 4
NDA, NH, NP = 4, 4, 4
Y_OUT_AT = LAG - 1
STATS_AT = {LAG + 1 + b: b for b in range(GB)}
PREP_AT = {
    0: {10: [("Z", 0)], 15: [("X", 0)], 16: [("U", 0)], 17: [("Z", 1)], 22: [("X", 1)], 23: [("U", 1)]},
    1: {6: [("E", 0)], 7: [("G", 0)], 12: [("R", 0)], 13: [("C", 0)], 14: [("Z", 0)], 19: [("X", 0)],
        20: [("U", 0)], 21: [("Z", 1)], 26: [("X", 1)], 27: [("U", 1)]},
}
W_MAX_AT = {3 * k + 1: k for k in range(KT)}
W_BC_AT = {27: 0, 29: 1}
W_EVERY = 2 * UNITS // KT
W_LOAD_AT = 2
W_ROUND_AT = {4: 0, 5: 1, 6: 2, 7: 3}
PROLOGUE = [("E", 0), ("G", 0), ("R", 0), ("C", 0), ("Z", 0), ("X", 0), ("U", 0), ("Z", 1), ("X", 1), ("U", 1)]
DIAGONAL = (4, 9, 14)
GATHER_AT = {21 + 2 * b: b for b in range(GB)}
SPLIT_AT, RSTD_AT = 2, 7
Z_AT = {h: {q: u for u, jobs in PREP_AT[h].items() for kind, q in jobs if kind == "Z"} for h in (0, 1)}
ACT_AFTER = 4


def slot_plan(h, first, prep):
    plan = []
    for u in range(UNITS):
        plan.append(("S", u))
        if first and u in W_BC_AT:
            plan.append(("M", W_BC_AT[u]))
        if prep:
            plan += PREP_AT[h].get(u, [])
    return plan


PLAN_FIRST = slot_plan(0, True, True)
PLAN = [slot_plan(0, False, True), slot_plan(1, False, True)]
PLAN_LAST = slot_plan(1, False, False)
EXTRA = len(PLAN_FIRST) - len(PLAN[0])
N0 = len(PROLOGUE)
NG = len(PLAN[0]) + len(PLAN[1])
assert EXTRA % 2 == 0 and N0 % 2 == 0 and NG % 2 == 0 and UNITS % NP == 0 and UNITS % NH == 0 and UNITS % NDA == 0


def static(g, value):
    return isinstance(g, int) and g == value


def slot_at(g, h, kind, arg):
    if static(g, 0) and h == 0:
        return PLAN_FIRST.index((kind, arg)) - EXTRA
    if static(g, GROUPS - 1) and h == 1:
        return len(PLAN[0]) + PLAN_LAST.index((kind, arg))
    return (len(PLAN[0]) if h else 0) + PLAN[h].index((kind, arg))


def slot_no(g, h, kind, arg):
    return g * NG + (N0 + EXTRA + slot_at(g, h, kind, arg))


def slot_side(g, h, kind, arg):
    return slot_at(g, h, kind, arg) % 2


def setup_stage(nc, d, s):
    with ExitStack() as ctx:
        sb = lambda name, shape, dt: ctx.enter_context(nc.sbuf_tensor(name, shape, dt))
        pb = lambda name, shape, dt: ctx.enter_context(nc.psum_tensor(name, shape, dt))
        sem = lambda name: ctx.enter_context(nc.semaphore(name))
        ids = sb("ids", [P, BATCH], I32)
        idf = sb("idf", [P, 3, BATCH], FP32)
        araw = sb("araw", [P, KT, STATE], FP32)
        drow = sb("drow", [RANK, DIM], FP32)
        usum = sb("usum", [RANK, 2], FP32)
        xpw = sb("xpw", [P, KT, XP], FP32)
        dtw = sb("dtw", [DTR, DIM], FP32)
        uct = sb("uct", [P, KT, RANK], FP32)
        mdt = sb("mdt", [DTR, RANK], FP32)
        w16 = sb("w16", [RANK, W_COLS], FP32)
        wide = sb("wide", [RANK * FOLD, W_COLS // FOLD], FP32)
        part = sb("part", [RANK * FOLD, 3, W_COLS // FOLD], BF16)
        p_ut = pb("p_ut", [P, 512], FP32)
        p_g = pb("p_g", [P, 512], FP32)
        p_bc = pb("p_bc", [P, 512], FP32)
        p_m = pb("p_mt", [P, 512], FP32)
        p_z = pb("p_z", [P, DIM], FP32)

        ids_in, u_in, a_in, w_in, d_in = (sem(n) for n in ("ids_in", "u_in", "a_in", "w_in", "d_in"))
        ident_ok, zero_ok, uc_ok, uct_done, uct_ok = (sem(n) for n in ("ident_ok", "zero_ok", "uc_ok", "uct_done", "uct_ok"))
        m_done, m_ok, z_done, part_ok, stacked = (sem(n) for n in ("m_done", "m_ok", "z_done", "part_ok", "stacked"))
        a_exp, dve_chain, idx_ok, w16_ok, wide_in = (sem(n) for n in ("a_exp", "dve_chain", "idx_ok", "w16_ok", "wide_in"))
        block = ctx.enter_context(nc.Block())

        @block.sync
        def _(sp):
            sp.dma_start(w16[:, W_H:W_H + DIM], d["lora_up"]).then_inc(u_in, 16)
            sp.dma_start(xpw[:, :, :], d["xp_wT"].rearrange("(k p) n -> p k n", p=P)).then_inc(w_in, 16)
            sp.dma_start(dtw[:, :], d["dt_wT"]).then_inc(w_in, 16)
            sp.dma_start(drow[:, :], d["D"].to_broadcast([RANK, DIM])).then_inc(d_in, 16)
            sp.dma_start(s["dtb"][:, :], d["dt_b"]).then_inc(d_in, 16)
            sp.wait_ge(w16_ok, 1)
            sp.dma_start(wide[:, :], w16[:, :].rearrange("r (f c) -> r f c", f=FOLD)).then_inc(wide_in, 16)
            for i in range(3):
                sp.wait_ge(part_ok, i + 1)
                for c, which in enumerate(WEIGHT_PARTS):
                    if which == i:
                        sp.dma_start(s["wst"][c * RANK:(c + 1) * RANK, :].rearrange("r (f c) -> r f c", f=FOLD),
                                     part[:, i, :]).then_inc(stacked, 16)
            sp.wait_ge(stacked, 16 * len(WEIGHT_PARTS))
            sp.wait_ge(d_in, 32)

        @block.gpsimd
        def _(pool):
            nc.gpsimd.memset(s["ident"][:, :], 0.0).then_inc(zero_ok, 1)
            pool.wait_ge(zero_ok, 1)
            nc.gpsimd.affine_select(out=s["ident"][:, :], in_=s["ident"][:, :], compare_op=ALU.not_equal, fill=1.0,
                                    base=0, pattern=[[-1, P]], channel_multiplier=1).then_inc(ident_ok, 1)
            pool.wait_ge(idx_ok, 1)
            nc.gpsimd.tensor_copy(s["idcur"][:, :], s["idx"][:, 0:GB]).then_inc(s["pool_chain"], 1)
            pool.wait_ge(s["pool_chain"], 1)
            for b in range(GB):
                nc.gpsimd.indirect_dma_start(
                    out=s["eraw"][:, b, :], out_offset=None, in_=d["lora_down"],
                    in_offset=bass.IndirectOffsetOnAxis(ap=s["idcur"][:, b:b + 1], axis=0)).then_inc(s["gathered"], 16)

        @block.scalar
        def _(act):
            act.dma_start(ids[:, :], d["x"]).then_inc(ids_in, 16)
            act.dma_start(araw[:, :, :], d["A_log"].rearrange("(k p) n -> p k n", p=P)).then_inc(a_in, 16)
            act.wait_ge(a_in, 16)
            nc.scalar.activation(s["aneg"][:, :, :], araw[:, :, :], ACT.Exp).then_inc(a_exp, 1)

        @block.tensor
        def _(pe):
            pe.wait_ge(ident_ok, 1)
            pe.wait_ge(uc_ok, 1)
            for k in range(KT):
                last = nc.tensor.transpose(p_ut[:, k * RANK:(k + 1) * RANK], w16[:, W_X + k * P:W_X + (k + 1) * P],
                                           s["ident"][0:RANK, 0:RANK])
            last.then_inc(uct_done, 1)
            pe.wait_ge(uct_ok, 1)
            pe.wait_ge(w_in, 32)
            for k in range(KT):
                nc.tensor.matmul(p_g[0:RANK, 0:RANK], uct[:, k, :], uct[:, k, :], start=k == 0, stop=k == KT - 1)
            for k in range(KT):
                nc.tensor.matmul(p_bc[0:RANK, 0:2 * STATE], uct[:, k, :], xpw[:, k, DTR:XP], start=k == 0, stop=k == KT - 1)
            for k in range(KT):
                last = nc.tensor.matmul(p_m[0:DTR, 0:RANK], xpw[:, k, 0:DTR], uct[:, k, :], start=k == 0, stop=k == KT - 1)
            last.then_inc(m_done, 1)
            pe.wait_ge(m_ok, 1)
            for j in range(2):
                last = nc.tensor.matmul(p_z[0:RANK, j * 512:(j + 1) * 512], mdt[:, :], dtw[:, j * 512:(j + 1) * 512],
                                        start=True, stop=True)
            last.then_inc(z_done, 1)

        @block.vector
        def _(dve):
            chain = [0]

            def link(ins):
                chain[0] += 1
                ins.then_inc(dve_chain, 1)
                dve.wait_ge(dve_chain, chain[0])

            dve.wait_ge(ids_in, 16)
            link(nc.vector.tensor_copy(idf[:, 0, :], ids[:, :]))
            link(nc.vector.tensor_scalar(idf[:, 1, :], idf[:, 0, :], 0.0, float(VOCAB), ALU.is_lt, ALU.mult))
            link(nc.vector.tensor_tensor(idf[:, 2, :], idf[:, 0, :], idf[:, 1, :], ALU.add))
            nc.vector.tensor_scalar(s["idx"][:, :], idf[:, 2, :], 0.0, float(VOCAB - 1), ALU.max, ALU.min).then_inc(idx_ok, 1)
            dve.wait_ge(u_in, 16)
            link(nc.vector.reduce_sum(usum[:, 0:1], w16[:, W_H:W_H + DIM], axis=AX.X))
            link(nc.vector.tensor_scalar(usum[:, 1:2], usum[:, 0:1], -1.0 / DIM, None, ALU.mult))
            nc.vector.tensor_scalar(w16[:, W_X:W_X + DIM], w16[:, W_H:W_H + DIM], usum[:, 1:2], None, ALU.add).then_inc(uc_ok, 1)
            dve.wait_ge(uct_done, 1)
            nc.vector.tensor_copy(uct[:, :, :], p_ut[:, 0:KT * RANK].rearrange("p (k n) -> p k n", k=KT)).then_inc(uct_ok, 1)
            dve.wait_ge(a_exp, 1)
            nc.vector.tensor_scalar(s["aneg"][:, :, :], s["aneg"][:, :, :], -1.0, None, ALU.mult)
            dve.wait_ge(d_in, 32)
            nc.vector.tensor_tensor(w16[:, W_D:W_D + DIM], w16[:, W_X:W_X + DIM], drow[:, :], ALU.mult)
            dve.wait_ge(m_done, 1)
            nc.vector.tensor_copy(mdt[:, :], p_m[0:DTR, 0:RANK]).then_inc(m_ok, 1)
            nc.vector.tensor_scalar(w16[:, W_G:W_G + RANK], p_g[0:RANK, 0:RANK], 1.0 / DIM, None, ALU.mult)
            nc.vector.tensor_copy(w16[:, W_BC:W_COLS], p_bc[0:RANK, 0:2 * STATE])
            dve.wait_ge(z_done, 1)
            nc.vector.tensor_copy(w16[:, W_Z:W_Z + DIM], p_z[0:RANK, :]).then_inc(w16_ok, 1)
            dve.wait_ge(wide_in, 16)
            nc.vector.tensor_copy(part[:, 0, :], wide[:, :]).then_inc(part_ok, 1)
            dve.wait_ge(part_ok, 1)
            link(nc.vector.tensor_tensor(wide[:, :], wide[:, :], part[:, 0, :], ALU.subtract))
            nc.vector.tensor_copy(part[:, 1, :], wide[:, :]).then_inc(part_ok, 1)
            dve.wait_ge(part_ok, 2)
            nc.vector.tensor_tensor(part[:, 2, :], wide[:, :], part[:, 1, :], ALU.subtract).then_inc(part_ok, 1)


def scan_stage(nc, d, s):
    with ExitStack() as ctx:
        sb = lambda name, shape, dt: ctx.enter_context(nc.sbuf_tensor(name, shape, dt))
        pb = lambda name, shape, dt: ctx.enter_context(nc.psum_tensor(name, shape, dt))
        sem = lambda name: ctx.enter_context(nc.semaphore(name))
        esc = sb("esc", [P, GB, RANK], FP32)
        erest = sb("erest", [P, GB, RANK], FP32)
        est = sb("est", [P, 2, GB, STACK], BF16)
        et = sb("et", [STACK, 2, GT], BF16)
        eg = sb("eg", [P, GB, RANK], FP32)
        vsum = sb("vsum", [P, GB], FP32)
        var = sb("var", [P, 5, GB], FP32)
        mhalf = sb("mhalf", [P, GB], FP32)
        c15 = sb("c15", [P, GB], FP32)
        one = sb("one", [P, 1], FP32)
        ct = sb("ct", [STATE, GT], FP32)
        identb = sb("identb1", [P, P], BF16)
        wabs = sb("wabs", [P, KT + 2], FP32)
        wk = sb("wk", [P, DIM], FP32)
        wexp = sb("wexp", [P, DIM], FP32)
        wrow = sb("wrow", [1, P], FP32)
        ones = sb("ones1", [1, P], FP32)
        bnext = sb("bnext", [P, GB, STATE], FP32)
        bcur = sb("bcur", [P, GB, STATE], FP32)
        cbc = sb("cbc", [P, STATE, GT], FP32)
        zb = sb("zb", [P, 2, GT], FP32)
        ez = sb("ez", [P, 2, GT], FP32)
        ux = sb("ux", [P, 2, GT], FP32)
        dtt = sb("dtt", [P, 2, HT, GT], FP32)
        ut = sb("u_tok", [P, 2, GB, HD], FP32)
        v = sb("v", [P, 2, GB, HD], FP32)
        da = sb("da", [P, NDA, 2, GT], FP32)
        hs = sb("hs", [P, NH, 2 * GT], FP32)
        ps = sb("ps", [P, NP, 2, GT], FP32)
        h2o = sb("h2o", [P, GB, HD], FP32)
        slot = pb("slot", [P, 2, 2 * GT], FP32)
        yp = pb("yp", [P, GB, HD], FP32)

        names = ("da_ready v_ready slot_full slot_read p_ready r_done y_read est_ready z_ready e_ready "
                 "sp_ready dt_ready var_ready bcur_ready h2_stored c_stored stats_done zero_ok").split()
        (da_ready, v_ready, slot_full, slot_read, p_ready, r_done, y_read, est_ready, z_ready, e_ready,
         sp_ready, dt_ready, var_ready, bcur_ready, h2_stored, c_stored, stats_done, zero_ok) = (sem(n) for n in names)
        dve_chain, eg_ok, mhalf_ok, w_in, wabs_done, wmax_col, ones_ok, wq_ok = (
            sem(n) for n in ("dve_chain1", "eg_ok", "mhalf_ok", "w_in1", "wabs_done", "wmax_col", "ones_ok1", "wq_ok"))
        pool_chain, gathered, eraw, idcur = (s[n] for n in ("pool_chain", "gathered", "eraw", "idcur"))
        c_loaded = [sem(f"c_loaded{c}") for c in range(4)]
        block = ctx.enter_context(nc.Block())
        h2v = d["h2"].rearrange("(b p) c -> p b c", p=P)
        wkv = d["ffn_wT"].rearrange("(k p) n -> k p n", p=P)
        ident, wst = s["ident"], s["wst"]
        CHAIN = 14
        def prep_slot(g, h, kind, arg):
            if isinstance(g, int) and g < 0:
                return PROLOGUE.index((kind, arg)), PROLOGUE.index((kind, arg)) % 2
            return slot_no(g, h, kind, arg), slot_side(g, h, kind, arg)

        def jobs(h, u, last):
            got = PREP_AT[h].get(u, [])
            return [] if last and h == 1 else got

        def z_no(g, h, q):
            return q if isinstance(g, int) and g < 0 else g * 4 + (2 + 2 * h + q)

        def unit_no(g, h, u):
            return g * (2 * UNITS) + (h * UNITS + u)

        def back(g, h, u, n):
            u -= n
            if u < 0:
                u += UNITS
                g, h = (g - 1, 1) if h == 0 else (g, 0)
            if isinstance(g, int) and g < 0:
                return None
            return g, h, u

        def groups(engine, body):
            body(0, False)
            with engine.Fori(1, GROUPS - 1) as g:
                body(g, False)
            body(GROUPS - 1, True)

        @block.sync
        def _(sp):
            def c_job(g, ahead):
                no, _ = prep_slot(g, 1, "C", 0)
                sp.wait_ge(slot_read, no + 1)
                sp.dma_start(d["c"][bass.ds(ahead, 1), :, :].rearrange("o n t -> (o n) t"),
                             ct[:, :]).then_inc(c_stored, 16)
                sp.wait_ge(c_stored, ahead * 16 + 16)
                for c in range(4):
                    if not (isinstance(g, int) and g < 0):
                        sp.wait_ge(p_ready, unit_no(g, 1, 8 * c + 7) + 1)
                    sp.dma_start(cbc[:, 4 * c:4 * c + 4, :],
                                 d["c"][bass.ds(ahead, 1), 4 * c:4 * c + 4, :].rearrange("o n t -> o (n t)")
                                 .to_broadcast([P, 4 * GT])).then_inc(c_loaded[c], 16)

            def h2_job(gp, hp):
                sp.wait_ge(y_read, gp * (2 * GB) + GB * (hp + 1))
                sp.dma_start(h2v[:, bass.ds(gp * GB, GB), hp * HD:(hp + 1) * HD], h2o[:, :, :]).then_inc(h2_stored, 16)

            def body(g, last):
                if not (isinstance(g, int) and g == 0):
                    h2_job(g - 1, 1)
                h2_job(g, 0)
                if not last:
                    c_job(g, g + 1)

            c_job(-1, 0)
            for k in range(KT):
                if k:
                    sp.wait_ge(wabs_done, k)
                sp.dma_start(wk[:, :], wkv[k]).then_inc(w_in, 16)
            groups(nc.sync, body)
            h2_job(GROUPS - 1, 1)
            sp.wait_ge(h2_stored, 16 * 2 * GROUPS)

        @block.gpsimd
        def _(pool):
            def ids_job(ahead):
                nc.gpsimd.tensor_copy(idcur[:, :], s["idx"][:, bass.ds(ahead * GB, GB)]).then_inc(pool_chain, 1)

            def gather(b):
                nc.gpsimd.indirect_dma_start(
                    out=eraw[:, b, :], out_offset=None, in_=d["lora_down"],
                    in_offset=bass.IndirectOffsetOnAxis(ap=idcur[:, b:b + 1], axis=0)).then_inc(gathered, 16)

            def split(src, i, ahead, c):
                at = ahead * CHAIN + c
                view = est[:, i, :, :].rearrange("p b (a r) -> p b a r", r=RANK)
                times = lambda x, n: x.unsqueeze(2).to_broadcast([P, GB, n, RANK])
                unit = lambda n: one[:, :].unsqueeze(2).unsqueeze(3).to_broadcast([P, GB, n, RANK])
                nc.gpsimd.tensor_tensor(view[:, :, 0:3, :], times(src, 3), unit(3), ALU.mult).then_inc(pool_chain, 1)
                pool.wait_ge(pool_chain, at + 1)
                nc.gpsimd.tensor_tensor(erest[:, :, :], src, view[:, :, 0, :], ALU.subtract).then_inc(pool_chain, 1)
                pool.wait_ge(pool_chain, at + 2)
                nc.gpsimd.tensor_tensor(view[:, :, 3:5, :], times(erest[:, :, :], 2), unit(2), ALU.mult).then_inc(pool_chain, 1)
                pool.wait_ge(pool_chain, at + 3)
                nc.gpsimd.tensor_tensor(view[:, :, 5, :], erest[:, :, :], view[:, :, 3, :], ALU.subtract).then_inc(est_ready, 1)
                pool.wait_ge(est_ready, ahead * 2 + (i + 1))

            def split_job(ahead):
                pool.wait_ge(gathered, ahead * (16 * GB) + 16 * GB)
                split(eraw[:, :, :], 0, ahead, 1)

            def rstd_job(ahead):
                at = ahead * CHAIN + 4
                pool.wait_ge(var_ready, ahead + 1)
                nc.gpsimd.tensor_tensor(var[:, 1, :], var[:, 0, :], mhalf[:, :], ALU.pow).then_inc(pool_chain, 1)
                pool.wait_ge(pool_chain, at + 1)
                nc.gpsimd.tensor_tensor(var[:, 2, :], var[:, 1, :], var[:, 1, :], ALU.mult).then_inc(pool_chain, 1)
                pool.wait_ge(pool_chain, at + 2)
                nc.gpsimd.tensor_tensor(var[:, 3, :], var[:, 2, :], var[:, 0, :], ALU.mult).then_inc(pool_chain, 1)
                pool.wait_ge(pool_chain, at + 3)
                nc.gpsimd.tensor_tensor(var[:, 2, :], var[:, 3, :], mhalf[:, :], ALU.mult).then_inc(pool_chain, 1)
                pool.wait_ge(pool_chain, at + 4)
                nc.gpsimd.tensor_tensor(var[:, 3, :], var[:, 2, :], c15[:, :], ALU.add).then_inc(pool_chain, 1)
                pool.wait_ge(pool_chain, at + 5)
                nc.gpsimd.tensor_tensor(var[:, 4, :], var[:, 3, :], var[:, 1, :], ALU.mult).then_inc(pool_chain, 1)
                pool.wait_ge(pool_chain, at + 6)
                nc.gpsimd.tensor_tensor(esc[:, :, :], eraw[:, :, :], var[:, 4, :].unsqueeze(2).to_broadcast([P, GB, RANK]),
                                        ALU.mult).then_inc(pool_chain, 1)
                pool.wait_ge(pool_chain, at + 7)
                split(esc[:, :, :], 1, ahead, 11)

            def cmul(g, h, n):
                u = 2 * n + 1
                if n % 4 == 0 and h == 0:
                    pool.wait_ge(c_loaded[n // 4], g * 16 + 16)
                pool.wait_ge(slot_read, slot_no(g, h, "S", u) + 1)
                b = back(g, h, u, NP)
                if b:
                    pool.wait_ge(r_done, unit_no(*b) + 1)
                nc.gpsimd.tensor_tensor(ps[:, (u - 1) % NP:(u - 1) % NP + 2, :, :].rearrange("p u j t -> p (u j) t"),
                                        hs[:, (u - 1) % NH:(u - 1) % NH + 2, :].rearrange("p u (j t) -> p (u j) t", j=2),
                                        cbc[:, n:n + 1, :].to_broadcast([P, 4, GT]), ALU.mult).then_inc(p_ready, 2)

            def body(g, last):
                for h in range(2):
                    for u in range(UNITS):
                        if h == 0 and u == min(GATHER_AT) and not last:
                            pool.wait_ge(pool_chain, g * CHAIN + (CHAIN + 1))
                        if u % 2 == 1:
                            cmul(g, h, u // 2)
                        if last:
                            continue
                        if h == 0 and u == min(GATHER_AT) - 1:
                            ids_job(g + 1)
                        if h == 0 and u in GATHER_AT:
                            gather(GATHER_AT[u])
                        if h == 1 and u == SPLIT_AT:
                            split_job(g + 1)
                        if h == 1 and u == RSTD_AT:
                            rstd_job(g + 1)

            nc.gpsimd.memset(mhalf[:, :], -0.5)
            nc.gpsimd.memset(one[:, :], 1.0)
            nc.gpsimd.memset(c15[:, :], 1.5).then_inc(mhalf_ok, 1)
            pool.wait_ge(mhalf_ok, 1)
            split_job(0)
            rstd_job(0)
            groups(nc.gpsimd, body)

        @block.scalar
        def _(act):
            def softplus_job(g, h, q):
                z = z_no(g, h, q)
                act.wait_ge(z_ready, z + 1)
                nc.scalar.activation(ez[:, :, :], ez[:, :, :], ACT.Exp).then_inc(e_ready, 1)
                act.wait_ge(e_ready, z + 1)
                nc.scalar.activation(ez[:, :, :], ez[:, :, :], ACT.Ln, bias=1.0).then_inc(sp_ready, 1)

            def b_mul(g, h, n):
                b = back(g, h, 2 * n, 4)
                if b:
                    act.wait_ge(slot_full, slot_no(b[0], b[1], "S", b[2] + 1) + 1)
                for i in range(GB):
                    if n in DIAGONAL:
                        m = nc.scalar.activation(v[:, n % 2, i, 0:P], ident[:, :], ACT.Copy, scale=bcur[:, i, n:n + 1])
                    else:
                        m = nc.scalar.activation(v[:, n % 2, i, :], ut[:, h, i, :], ACT.Copy, scale=bcur[:, i, n:n + 1])
                m.then_inc(v_ready, 1)

            def exp_a(g, h, u):
                n, q = u // 2, u % 2
                b = back(g, h, u, NDA)
                if b:
                    act.wait_ge(slot_read, slot_no(b[0], b[1], "S", b[2]) + 1)
                for j in range(2):
                    t = 2 * q + j
                    m = nc.scalar.activation(
                        da[:, u % NDA, j, :].rearrange("p (b t) -> p b t", b=GB)[:, :, 1:SEQ],
                        dtt[:, h, t, :].rearrange("p (b t) -> p b t", b=GB)[:, :, 1:SEQ],
                        ACT.Exp, scale=s["aneg"][:, h * HT + t, n:n + 1])
                m.then_inc(da_ready, 1)

            def body(g, last):
                for h in range(2):
                    if h == 0:
                        no = slot_no(g - 1, 1, "C", 0) if not isinstance(g, int) or g > 0 else PROLOGUE.index(("C", 0))
                        act.wait_ge(slot_read, no + 1)
                        if not static(g, 0):
                            act.wait_ge(v_ready, g * (2 * STATE))
                        nc.scalar.activation(bcur[:, :, :], bnext[:, :, :], ACT.Copy).then_inc(bcur_ready, 1)
                        act.wait_ge(bcur_ready, g + 1)
                    if h == 1:
                        no = slot_no(g, 0, "U", 1)
                    else:
                        no = slot_no(g - 1, 1, "U", 1) if not isinstance(g, int) or g > 0 else PROLOGUE.index(("U", 1))
                    act.wait_ge(slot_read, no + 1)
                    for u in range(UNITS):
                        if u % 2 == 0:
                            b_mul(g, h, u // 2)
                        exp_a(g, h, u)
                        if last and u % W_EVERY == W_LOAD_AT:
                            k = (h * UNITS + u) // W_EVERY
                            act.wait_ge(*((wq_ok, k) if k else (wabs_done, KT)))
                            act.dma_start(wk[:, :], wkv[k]).then_inc(w_in, 16)
                        if last and h == 1:
                            continue
                        for q in range(2):
                            if u == Z_AT[h][q] + ACT_AFTER:
                                softplus_job(g, h, q)

            nc.scalar.preload_act_table_set("natural_log_exp_and_others")
            for q in range(2):
                softplus_job(-1, 1, q)
            act.wait_ge(zero_ok, 1)
            groups(nc.scalar, body)

        @block.tensor
        def _(pe):
            def free_slot(no):
                if isinstance(no, int) and no < 2:
                    return
                pe.wait_ge(slot_read, no - 1)

            def trans(g, h, u):
                n, q = u // 2, u % 2
                no, side = slot_no(g, h, "S", u), slot_side(g, h, "S", u)
                free_slot(no)
                if q == 0:
                    pe.wait_ge(v_ready, g * (2 * STATE) + (h * STATE + n + 1))
                for j in range(2):
                    for b in range(GB):
                        c = (2 * q + j) * P
                        to = slot[:, side, j * GT + b * P:j * GT + (b + 1) * P]
                        if n in DIAGONAL:
                            m = nc.tensor.matmul(to, ut[:, h, b, c:c + P], v[:, n % 2, b, 0:P], start=True, stop=True)
                        else:
                            m = nc.tensor.transpose(to, v[:, n % 2, b, c:c + P], ident[:, :])
                m.then_inc(slot_full, 1)

            def reduce_n(g, h, u):
                q = u % 2
                pe.wait_ge(p_ready, unit_no(g, h, u) + 1)
                for j in range(2):
                    c = (2 * q + j) * P
                    for b in range(GB):
                        m = nc.tensor.matmul(yp[:, b, c:c + P], ps[:, u % NP, j, b * P:(b + 1) * P], ident[:, :],
                                             start=False, stop=u == UNITS - 1 and j == 1, is_transpose=True)
                m.then_inc(r_done, 1)

            def residual(g, h):
                for b in range(GB):
                    if not (isinstance(g, int) and g == 0 and h == 0):
                        pe.wait_ge(y_read, g * (2 * GB) + (GB * h - GB + b + 1))
                    nc.tensor.matmul(yp[:, b, :], et[:, 0, b * P:(b + 1) * P], wst[:, W_H + h * HD:W_H + (h + 1) * HD],
                                     start=True, stop=False)
                    nc.tensor.matmul(yp[:, b, :], et[:, 1, b * P:(b + 1) * P], wst[:, W_D + h * HD:W_D + (h + 1) * HD],
                                     start=False, stop=False)

            def max_turn(i):
                no, side = slot_no(0, 0, "M", i), slot_side(0, 0, "M", i)
                free_slot(no)
                if i == 0:
                    pe.wait_ge(wmax_col, 1)
                    nc.tensor.transpose(slot[0:1, side, 0:P], wabs[:, KT:KT + 1], ident[:, :]).then_inc(slot_full, 1)
                else:
                    pe.wait_ge(slot_read, slot_no(0, 0, "M", 0) + 1)
                    nc.tensor.matmul(slot[:, side, 0:1], ones[0:1, :], wrow[0:1, 0:1], start=True, stop=True).then_inc(slot_full, 1)

            def prep(g, h, kind, arg, ahead):
                no, side = prep_slot(g, h, kind, arg)
                free_slot(no)
                if kind in "ER":
                    i = int(kind == "R")
                    pe.wait_ge(est_ready, ahead * 2 + (i + 1))
                    half = slot[:, side, :].bitcast(BF16)
                    for b in range(GB):
                        m = nc.tensor.transpose(half[0:STACK, b * P:(b + 1) * P], est[:, i, b, :], identb[:, :])
                if kind == "G":
                    pe.wait_ge(slot_read, prep_slot(g, h, "E", 0)[0] + 1)
                    for b in range(GB):
                        m = nc.tensor.matmul(slot[:, side, b * RANK:(b + 1) * RANK], et[:, 0, b * P:(b + 1) * P],
                                             wst[:, W_G:W_G + RANK], start=True, stop=True)
                if kind == "C":
                    pe.wait_ge(slot_read, prep_slot(g, h, "R", 0)[0] + 1)
                    nc.tensor.matmul(slot[0:STATE, side, 0:GT], wst[:, W_BC + STATE:W_COLS], et[:, 1, :], start=True, stop=True)
                    for b in range(GB):
                        m = nc.tensor.matmul(slot[:, side, GT + b * STATE:GT + (b + 1) * STATE], et[:, 1, b * P:(b + 1) * P],
                                             wst[:, W_BC:W_BC + STATE], start=True, stop=True)
                if kind in "ZX":
                    for j in range(2):
                        c = (W_Z if kind == "Z" else W_X) + ((1 - h) * HT + 2 * arg + j) * P
                        m = nc.tensor.matmul(slot[:, side, j * GT:(j + 1) * GT], wst[:, c:c + P], et[:, 1, :],
                                             start=True, stop=True)
                if kind == "U":
                    pe.wait_ge(slot_read, prep_slot(g, h, "X", arg)[0] + 1)
                    for b in range(GB):
                        for j in range(2):
                            m = nc.tensor.transpose(slot[:, side, (b * 2 + j) * P:(b * 2 + j + 1) * P],
                                                    ux[:, j, b * P:(b + 1) * P], ident[:, :])
                m.then_inc(slot_full, 1)

            def body(g, last):
                for h in range(2):
                    first = isinstance(g, int) and g == 0 and h == 0
                    for u in range(UNITS):
                        trans(g, h, u)
                        if u == LAG:
                            residual(g, h)
                        b = back(g, h, u, LAG)
                        if b:
                            reduce_n(*b)
                        if first and u in W_BC_AT:
                            max_turn(W_BC_AT[u])
                        for kind, arg in jobs(h, u, last):
                            prep(g, h, kind, arg, g + 1)

            pe.wait_ge(ones_ok, 1)
            for kind, arg in PROLOGUE:
                prep(-1, 1, kind, arg, 0)
            groups(nc.tensor, body)
            for u in range(UNITS - LAG, UNITS):
                reduce_n(GROUPS - 1, 1, u)

        @block.vector
        def _(dve):
            chain = [0]

            def link(ins):
                chain[0] += 1
                ins.then_inc(dve_chain, 1)
                dve.wait_ge(dve_chain, chain[0])

            def weight_max(k):
                dve.wait_ge(w_in, 16 * (k + 1))
                nc.vector.tensor_reduce(wabs[:, k:k + 1], wk[:, :], AX.X, ALU.max, apply_absolute_value=True).then_inc(wabs_done, 1)
                if k == KT - 1:
                    dve.wait_ge(wabs_done, KT)
                    nc.vector.reduce_max(wabs[:, KT:KT + 1], wabs[:, 0:KT], axis=AX.X).then_inc(wmax_col, 1)

            def max_out(i):
                no, side = slot_no(0, 0, "M", i), slot_side(0, 0, "M", i)
                dve.wait_ge(slot_full, no + 1)
                if i == 0:
                    nc.vector.reduce_max(wrow[0:1, 0:1], slot[0:1, side, 0:P], axis=AX.X).then_inc(slot_read, 1)
                else:
                    nc.vector.tensor_scalar(s["winv"][:, :], slot[:, side, 0:1], 1e-12, 1.0 / FP8_MAX, ALU.max,
                                            ALU.mult).then_inc(slot_read, 1)
                    dve.wait_ge(slot_read, no + 1)
                    nc.vector.reciprocal(wabs[:, KT + 1:KT + 2], s["winv"][:, :])

            def round_weight(k, step):
                if step == 0:
                    dve.wait_ge(w_in, 16 * (KT + k + 1))
                    link(nc.vector.tensor_scalar(wk[:, :], wk[:, :], wabs[:, KT + 1:KT + 2], None, ALU.mult))
                if step == 1:
                    link(nc.vector.tensor_scalar(wexp[:, :].bitcast(I32), wk[:, :].bitcast(I32), EXP_BITS, None, ALU.bitwise_and))
                    link(nc.vector.tensor_scalar(wexp[:, :], wexp[:, :], MIN_NORMAL, ROUND, ALU.max, ALU.mult))
                if step == 2:
                    link(nc.vector.tensor_tensor(wk[:, :], wk[:, :], wexp[:, :], ALU.add))
                if step == 3:
                    nc.vector.tensor_tensor(s["wq"][:, k, :], wk[:, :], wexp[:, :], ALU.subtract).then_inc(wq_ok, 1)

            def scan(g, h, u):
                no, side = slot_no(g, h, "S", u), slot_side(g, h, "S", u)
                dve.wait_ge(da_ready, unit_no(g, h, u) + 1)
                dve.wait_ge(slot_full, no + 1)
                b = back(g, h, u, NH)
                if b:
                    dve.wait_ge(p_ready, unit_no(*b) + 1)
                nc.vector.tensor_tensor_scan(hs[:, u % NH, :], da[:, u % NDA, :, :].rearrange("p j t -> p (j t)"),
                                             slot[:, side, :], 0.0, ALU.mult, ALU.add).then_inc(slot_read, 1)

            def y_out(g, h):
                dve.wait_ge(r_done, unit_no(g, h, UNITS - 1) + 1)
                if not (static(g, 0) and h == 0):
                    dve.wait_ge(h2_stored, g * 32 + 16 * h)
                    dve.wait_ge(stats_done, g * (2 * GB) + GB * h)
                for b in range(GB):
                    nc.vector.tensor_scalar(h2o[:, b, :], yp[:, b, :], 1.0, None, ALU.mult, ALU.max,
                                            accum_out=s["hmax"][:, bass.ds(g * GB + b, 1), h]).then_inc(y_read, 1)

            def h2_stats(g, h, b):
                dve.wait_ge(y_read, g * (2 * GB) + (GB * h + b + 1))
                nc.vector.bn_stats(s["stats"][:, bass.ds(g * GB + b, 1), h, :].rearrange("p o f -> p (o f)"), h2o[:, b, :])
                nc.vector.tensor_reduce(s["hmin"][:, bass.ds(g * GB + b, 1), h], h2o[:, b, :], AX.X,
                                        ALU.min).then_inc(stats_done, 1)

            def prep(g, h, kind, arg, ahead):
                no, side = prep_slot(g, h, kind, arg)
                dve.wait_ge(slot_full, no + 1)
                if kind in "ER":
                    m = nc.vector.tensor_copy(et[:, int(kind == "R"), :], slot[:, side, :].bitcast(BF16)[0:STACK, 0:GT])
                if kind == "G":
                    nc.vector.tensor_tensor(eg[:, :, :], slot[:, side, 0:GB * RANK].rearrange("p (b n) -> p b n", b=GB),
                                            eraw[:, :, :], ALU.mult).then_inc(slot_read, 1)
                    dve.wait_ge(slot_read, no + 1)
                    nc.vector.reduce_sum(vsum[:, :], eg[:, :, :], axis=AX.X).then_inc(eg_ok, 1)
                    dve.wait_ge(eg_ok, ahead + 1)
                    nc.vector.tensor_scalar(var[:, 0, :], vsum[:, :], 0.0, EPS, ALU.max, ALU.add).then_inc(var_ready, 1)
                    return
                if kind == "C":
                    if not static(g, -1):
                        dve.wait_ge(c_stored, ahead * 16)
                        dve.wait_ge(bcur_ready, ahead)
                    nc.vector.tensor_copy(bnext[:, :, :], slot[:, side, GT:GT + GB * STATE].rearrange("p (b n) -> p b n", b=GB))
                    m = nc.vector.tensor_copy(ct[:, :], slot[0:STATE, side, 0:GT])
                if kind == "Z":
                    z = z_no(g, h, arg)
                    if not (isinstance(z, int) and z == 0):
                        dve.wait_ge(dt_ready, z)
                    for j in range(2):
                        k = (1 - h) * HT + 2 * arg + j
                        m = nc.vector.tensor_scalar(zb[:, j, :], slot[:, side, j * GT:(j + 1) * GT],
                                                    s["dtb"][:, k:k + 1], None, ALU.add)
                    m.then_inc(slot_read, 1)
                    dve.wait_ge(slot_read, no + 1)
                    nc.vector.tensor_scalar(ez[:, :, :], zb[:, :, :], 30.0, None, ALU.min).then_inc(z_ready, 1)
                    return
                if kind == "X":
                    z = z_no(g, h, arg)
                    dve.wait_ge(sp_ready, z + 1)
                    nc.vector.tensor_tensor(dtt[:, 1 - h, 2 * arg:2 * arg + 2, :], zb[:, :, :], ez[:, :, :],
                                            ALU.max).then_inc(dt_ready, 1)
                    dve.wait_ge(dt_ready, z + 1)
                    m = nc.vector.tensor_tensor(ux[:, :, :], slot[:, side, :].rearrange("p (j t) -> p j t", j=2),
                                                dtt[:, 1 - h, 2 * arg:2 * arg + 2, :], ALU.mult)
                if kind == "U":
                    m = nc.vector.tensor_copy(ut[:, 1 - h, :, arg * 2 * P:(arg + 1) * 2 * P],
                                              slot[:, side, :].rearrange("p (b c) -> p b c", b=GB))
                m.then_inc(slot_read, 1)

            def body(g, last):
                for h in range(2):
                    first = isinstance(g, int) and g == 0 and h == 0
                    gp, hp = (g - 1, 1) if h == 0 else (g, 0)
                    for u in range(UNITS):
                        scan(g, h, u)
                        if not first and u == Y_OUT_AT:
                            y_out(gp, hp)
                        if not first and u in STATS_AT:
                            h2_stats(gp, hp, STATS_AT[u])
                        if first and u in W_MAX_AT:
                            weight_max(W_MAX_AT[u])
                        if first and u in W_BC_AT:
                            max_out(W_BC_AT[u])
                        if last and u % W_EVERY in W_ROUND_AT:
                            round_weight((h * UNITS + u) // W_EVERY, W_ROUND_AT[u % W_EVERY])
                        for kind, arg in jobs(h, u, last):
                            prep(g, h, kind, arg, g + 1)

            nc.vector.tensor_copy(identb[:, :], ident[:, :])
            nc.vector.memset(ones[:, :], 1.0).then_inc(ones_ok, 1)
            for c in range(NDA):
                z0 = nc.vector.memset(da[:, c, :, :].rearrange("p j (b t) -> p (j b) t", t=SEQ)[:, :, 0:1], 0.0)
            z0.then_inc(zero_ok, 1)
            for kind, arg in PROLOGUE:
                prep(-1, 1, kind, arg, 0)
            groups(nc.vector, body)
            y_out(GROUPS - 1, 1)
            for b in range(GB):
                h2_stats(GROUPS - 1, 1, b)


def ffn_stage(nc, d, s):
    with ExitStack() as ctx:
        sb = lambda name, shape, dt: ctx.enter_context(nc.sbuf_tensor(name, shape, dt))
        pb = lambda name, shape, dt: ctx.enter_context(nc.psum_tensor(name, shape, dt))
        sem = lambda name: ctx.enter_context(nc.semaphore(name))
        UN = 8
        OP = 4
        TURNS = BATCH // UN
        ms = sb("ms", [P, 4, BATCH], FP32)
        dev = sb("dev", [P, BATCH, 4], FP32)
        mean = sb("mean", [P, BATCH], FP32)
        std = sb("std", [P, BATCH], FP32)
        rstd = sb("rstd", [P, BATCH], FP32)
        ext = sb("ext", [P, 2, BATCH], FP32)
        sc = sb("sc", [P, BATCH], FP32)
        nb = sb("nb", [P, BATCH], FP32)
        cm = sb("cm", [P, 4], FP32)
        row = sb("row2", [1, P], FP32)
        ones = sb("ones2", [1, P], FP32)
        identb = sb("identb", [P, P], BF16)
        wq = s["wq"]
        brow = sb("brow", [1, 2, DIM], FP32)
        bpart = sb("bpart", [1, 3, DIM], BF16)
        bst = sb("bst", [3, DIM], BF16)
        ones3 = sb("ones3", [3, P], BF16)
        h2 = sb("h2_in", [P, UN, DIM], FP32)
        v = sb("v2", [P, 2, DIM], FP32)
        e = sb("e2", [P, DIM], FP32)
        m = sb("m2", [P, 2, DIM], FP32)
        w = sb("w2", [P, 2, DIM], FP32)
        q = sb("q2", [P, 2, DIM], BF16)
        qt = sb("qt", [P, 2, KT, P], BF16)
        o = sb("o", [P, OP, DIM], FP32)
        p_m = pb("p_m", [P, 512], FP32)
        qp = pb("qp", [P, 2, KT * P], BF16)
        acc = pb("acc", [P, 2, DIM], FP32)
        names = ("identb_ok bias_in var_ok std_ok cm_ok row_done max_ok bc_done ones_ok scale_ok dve_chain "
                 "v_ready q_ready qp_ready qt_ready acc_ready o_ready").split()
        (identb_ok, bias_in, var_ok, std_ok, cm_ok, row_done, max_ok, bc_done, ones_ok, scale_ok, dve_chain,
         v_ready, q_ready, qp_ready, qt_ready, acc_ready, o_ready) = (sem("f_" + n) for n in names)
        h2_in = [sem(f"f_h2_in{j}") for j in range(UN)]
        o_out = [sem(f"f_o_out{j}") for j in range(OP)]
        e_done = sem("f_e_done")
        m_ready, w_ready, bpart_ok, bst_in, ones3_ok = (sem("f_" + n) for n in ("m_ready", "w_ready", "bpart_ok", "bst_in", "ones3_ok"))
        block = ctx.enter_context(nc.Block())
        h2v = d["h2"].rearrange("(b p) c -> p b c", p=P)
        ov = d["out"].rearrange("(b p) c -> p b c", p=P)

        def turns(engine, body):
            body(0)
            with engine.Fori(1, TURNS) as i:
                body(i)

        @block.sync
        def _(sp):
            sp.dma_start(brow[:, 0, :], d["ffn_b"]).then_inc(bias_in, 16)
            sp.wait_ge(bpart_ok, 1)
            for i in range(3):
                sp.dma_start(bst[i:i + 1, :], bpart[:, i, :]).then_inc(bst_in, 16)

            def body(i):
                for j in range(UN):
                    sp.wait_ge(o_ready, i * UN + (j + 1))
                    sp.dma_start(ov[:, bass.ds(i * UN + j, 1), :].rearrange("p o c -> p (o c)"), o[:, j % OP, :]).then_inc(o_out[j % OP], 16)

            turns(nc.sync, body)
            for j in range(OP):
                sp.wait_ge(o_out[j], 16 * (BATCH // OP))

        @block.gpsimd
        def _(pool):
            def body(i):
                for j in range(UN):
                    pool.wait_ge(m_ready, i * UN + (j + 1))
                    if not (static(i, 0) and j < 2):
                        pool.wait_ge(q_ready, i * UN + (j - 1))
                    nc.gpsimd.tensor_tensor(w[:, j % 2, :], v[:, j % 2, :], m[:, j % 2, :], ALU.add).then_inc(w_ready, 1)

            turns(nc.gpsimd, body)

        @block.scalar
        def _(act):
            def load(i, j):
                act.dma_start(h2[:, j, :], h2v[:, bass.ds(i * UN + j, 1), :].rearrange("p o c -> p (o c)")).then_inc(h2_in[j], 16)

            for j in range(4):
                load(0, j)
            act.wait_ge(var_ok, 1)
            nc.scalar.activation(std[:, :], ms[:, 1, :], ACT.Sqrt).then_inc(std_ok, 1)
            act.wait_ge(scale_ok, 1)

            def qt_copy(i, j):
                act.wait_ge(qp_ready, i * UN + (j + 1))
                if not (static(i, 0) and j < 2):
                    act.wait_ge(acc_ready, i * UN + (j - 1))
                nc.scalar.activation(qt[:, j % 2, :, :], qp[:, j % 2, :].rearrange("p (k t) -> p k t", k=KT),
                                     ACT.Copy).then_inc(qt_ready, 1)

            def body(i, last=False):
                for j in range(UN):
                    act.wait_ge(h2_in[j], i * 16 + 16)
                    if not (static(i, 0) and j < 2):
                        act.wait_ge(w_ready, i * UN + (j - 1))
                    nc.scalar.activation(v[:, j % 2, :], h2[:, j, :], ACT.Identity, bias=nb[:, bass.ds(i * UN + j, 1)],
                                         scale=sc[:, bass.ds(i * UN + j, 1)]).then_inc(v_ready, 1)
                    if not (static(i, 0) and j < 2):
                        qt_copy(*((i, j - 2) if j >= 2 else (i - 1, j + UN - 2)))
                    if not (static(i, 0) and j < 4):
                        act.wait_ge(o_ready, i * UN + (j - 3))
                    if j < 4:
                        load(i, j + 4)
                    elif not last:
                        load(i + 1, j - 4)

            def first_and_last(body):
                body(0)
                with nc.scalar.Fori(1, TURNS - 1) as i:
                    body(i)
                body(TURNS - 1, True)

            first_and_last(body)
            qt_copy(TURNS - 1, UN - 2)
            qt_copy(TURNS - 1, UN - 1)

        @block.tensor
        def _(pe):
            pe.wait_ge(cm_ok, 1)
            nc.tensor.transpose(p_m[0:1, 0:P], cm[:, 0:1], s["ident"][:, :]).then_inc(row_done, 1)
            pe.wait_ge(ones_ok, 1)
            pe.wait_ge(max_ok, 1)
            nc.tensor.matmul(p_m[:, P:P + 1], ones[0:1, :], row[0:1, 0:1], start=True, stop=True).then_inc(bc_done, 1)
            pe.wait_ge(identb_ok, 1)

            def transposes(i, j):
                pe.wait_ge(q_ready, i * UN + (j + 1))
                if not (static(i, 0) and j < 2):
                    pe.wait_ge(qt_ready, i * UN + (j - 1))
                for k in range(KT):
                    t = nc.tensor.transpose(qp[:, j % 2, k * P:(k + 1) * P], q[:, j % 2, k * P:(k + 1) * P], identb[:, :])
                t.then_inc(qp_ready, 1)

            def products(i, j):
                pe.wait_ge(qt_ready, i * UN + (j + 1))
                if not (static(i, 0) and j < 2):
                    pe.wait_ge(o_ready, i * UN + (j - 1))
                for n in range(2):
                    for k in range(KT):
                        nc.tensor.matmul(acc[:, j % 2, n * HD:(n + 1) * HD], qt[:, j % 2, k, :],
                                         wq[:, k, n * HD:(n + 1) * HD], start=k == 0, stop=False)
                    if static(i, 0) and j == 0 and n == 0:
                        pe.wait_ge(bst_in, 48)
                        pe.wait_ge(ones3_ok, 1)
                    t = nc.tensor.matmul(acc[:, j % 2, n * HD:(n + 1) * HD], ones3[:, :], bst[:, n * HD:(n + 1) * HD],
                                         start=False, stop=True)
                t.then_inc(acc_ready, 1)

            def body(i):
                for j in range(UN):
                    transposes(i, j)
                    if not (static(i, 0) and j == 0):
                        products(*((i, j - 1) if j else (i - 1, UN - 1)))

            turns(nc.tensor, body)
            products(TURNS - 1, UN - 1)

        @block.vector
        def _(dve):
            chain = [0]

            def link(ins):
                chain[0] += 1
                ins.then_inc(dve_chain, 1)
                dve.wait_ge(dve_chain, chain[0])

            part = s["stats"][:, :, :, :].rearrange("p b h (a c) -> p b (h a) c", c=3)
            link(nc.vector.reduce_sum(ms[:, 0, :], part[:, :, :, 1], axis=AX.X))
            link(nc.vector.tensor_scalar(mean[:, :], ms[:, 0, :], 0.25, None, ALU.mult))
            link(nc.vector.tensor_tensor(dev[:, :, :], part[:, :, :, 1],
                                         mean[:, :].unsqueeze(2).to_broadcast([P, BATCH, 4]), ALU.subtract))
            link(nc.vector.tensor_tensor(dev[:, :, :], dev[:, :, :], dev[:, :, :], ALU.mult))
            link(nc.vector.scalar_tensor_tensor(dev[:, :, :], dev[:, :, :], DIM / 4.0, part[:, :, :, 2], ALU.mult, ALU.add))
            link(nc.vector.reduce_sum(ms[:, 0, :], dev[:, :, :], axis=AX.X))
            nc.vector.tensor_scalar(ms[:, 1, :], ms[:, 0, :], 1.0 / DIM, EPS, ALU.mult, ALU.add).then_inc(var_ok, 1)
            dve.wait_ge(std_ok, 1)
            link(nc.vector.reciprocal(rstd[:, :], std[:, :]))
            link(nc.vector.tensor_tensor(ext[:, 0, :], s["hmax"][:, :, 0], s["hmax"][:, :, 1], ALU.max))
            link(nc.vector.tensor_tensor(ext[:, 1, :], s["hmin"][:, :, 0], s["hmin"][:, :, 1], ALU.min))
            link(nc.vector.tensor_tensor(ext[:, 0, :], ext[:, 0, :], mean[:, :], ALU.subtract))
            link(nc.vector.tensor_tensor(ext[:, 1, :], mean[:, :], ext[:, 1, :], ALU.subtract))
            link(nc.vector.tensor_tensor(ext[:, 0, :], ext[:, 0, :], ext[:, 1, :], ALU.max))
            link(nc.vector.tensor_tensor(ext[:, 0, :], ext[:, 0, :], rstd[:, :], ALU.mult))
            nc.vector.reduce_max(cm[:, 0:1], ext[:, 0, :], axis=AX.X).then_inc(cm_ok, 1)
            nc.vector.memset(ones[:, :], 1.0).then_inc(ones_ok, 1)
            nc.vector.tensor_copy(identb[:, :], s["ident"][:, :]).then_inc(identb_ok, 1)
            dve.wait_ge(row_done, 1)
            nc.vector.reduce_max(row[0:1, 0:1], p_m[0:1, 0:P], axis=AX.X).then_inc(max_ok, 1)
            dve.wait_ge(bc_done, 1)
            link(nc.vector.tensor_scalar(cm[:, 1:2], p_m[:, P:P + 1], 1e-12, 1.0 / FP8_MAX, ALU.max, ALU.mult))
            link(nc.vector.reciprocal(cm[:, 2:3], cm[:, 1:2]))
            link(nc.vector.tensor_tensor(cm[:, 3:4], cm[:, 1:2], s["winv"][:, :], ALU.mult))
            link(nc.vector.tensor_scalar(sc[:, :], rstd[:, :], cm[:, 2:3], None, ALU.mult))
            nc.vector.scalar_tensor_tensor(nb[:, :], mean[:, :], -1.0, sc[:, :], ALU.mult, ALU.mult).then_inc(scale_ok, 1)

            def bias_parts():
                nc.vector.memset(ones3[:, :], 1.0).then_inc(ones3_ok, 1)
                link(nc.vector.reciprocal(cm[:, 2:3], cm[:, 3:4]))
                dve.wait_ge(bias_in, 16)
                link(nc.vector.tensor_scalar(brow[:, 0, :], brow[:, 0, :], cm[0:1, 2:3], None, ALU.mult))
                link(nc.vector.tensor_copy(bpart[:, 0, :], brow[:, 0, :]))
                link(nc.vector.tensor_tensor(brow[:, 1, :], brow[:, 0, :], bpart[:, 0, :], ALU.subtract))
                link(nc.vector.tensor_copy(bpart[:, 1, :], brow[:, 1, :]))
                nc.vector.tensor_tensor(bpart[:, 2, :], brow[:, 1, :], bpart[:, 1, :], ALU.subtract).then_inc(bpart_ok, 1)

            def exponent(i, j):
                dve.wait_ge(v_ready, i * UN + (j + 1))
                if not (static(i, 0) and j == 0):
                    dve.wait_ge(m_ready, i * UN + j)
                nc.vector.tensor_scalar(e[:, :].bitcast(I32), v[:, j % 2, :].bitcast(I32), EXP_BITS, None,
                                        ALU.bitwise_and).then_inc(e_done, 1)

            def constant(i, j):
                dve.wait_ge(e_done, i * UN + (j + 1))
                nc.vector.tensor_scalar(m[:, j % 2, :], e[:, :], MIN_NORMAL, ROUND, ALU.max, ALU.mult).then_inc(m_ready, 1)

            def rounded(i, j):
                dve.wait_ge(w_ready, i * UN + (j + 1))
                if not (static(i, 0) and j < 2):
                    dve.wait_ge(qp_ready, i * UN + (j - 1))
                nc.vector.tensor_tensor(q[:, j % 2, :], w[:, j % 2, :], m[:, j % 2, :], ALU.subtract).then_inc(q_ready, 1)

            def output(i, j):
                dve.wait_ge(acc_ready, i * UN + (j + 1))
                if not (static(i, 0) and j < OP):
                    dve.wait_ge(o_out[j % OP], i * (16 * UN // OP) + 16 * (j // OP))
                nc.vector.scalar_tensor_tensor(o[:, j % OP, :], acc[:, j % 2, :], cm[:, 3:4], h2[:, j, :],
                                               ALU.mult, ALU.add).then_inc(o_ready, 1)

            def body(i):
                for j in range(UN):
                    exponent(i, j)
                    if not (static(i, 0) and j < 1):
                        gi, gj = (i, j - 1) if j >= 1 else (i - 1, UN - 1)
                        rounded(gi, gj)
                    constant(i, j)
                    if static(i, 0) and j == 0:
                        bias_parts()
                    if not (static(i, 0) and j < 3):
                        gi, gj = (i, j - 3) if j >= 3 else (i - 1, j + UN - 3)
                        output(gi, gj)

            turns(nc.vector, body)
            rounded(TURNS - 1, UN - 1)
            output(TURNS - 1, UN - 3)
            output(TURNS - 1, UN - 2)
            output(TURNS - 1, UN - 1)


def build(nc, d):
    d["h2"] = nc.dram_tensor("h2_scratch", (BATCH * SEQ, DIM), FP32, kind="Internal").ap()
    d["c"] = nc.dram_tensor("c_scratch", (GROUPS, STATE, GT), FP32, kind="Internal").ap()
    with ExitStack() as ctx:
        s = {}
        for name, shape, dt in (
                ("ident", [P, P], FP32),
                ("winv", [P, 1], FP32),
                ("stats", [P, BATCH, 2, 6], FP32),
                ("hmax", [P, BATCH, 2], FP32),
                ("hmin", [P, BATCH, 2], FP32),
                ("idcur", [P, GB], U32),
                ("eraw", [P, GB, RANK], FP32),
                ("idx", [P, BATCH], U32),
                ("wst", [STACK, W_COLS], BF16),
                ("wq", [P, KT, DIM], BF16),
                ("dtb", [P, KT], FP32),
                ("aneg", [P, KT, STATE], FP32)):
            s[name] = ctx.enter_context(nc.sbuf_tensor("s_" + name, shape, dt))
        for name in ("pool_chain", "gathered"):
            s[name] = ctx.enter_context(nc.semaphore(name))
        setup_stage(nc, d, s)
        scan_stage(nc, d, s)
        ffn_stage(nc, d, s)


def kernel(x, L0_tok_lora_down, L0_tok_lora_up, L0_attn_A_log, L0_attn_D, L0_attn_x_proj_w, L0_attn_dt_proj_w,
           L0_attn_dt_proj_b, L0_ffn_weight, L0_ffn_bias):
    import numpy as np
    import concourse.bacc as bacc
    from concourse.bass_utils import run_bass_kernel_spmd

    arrays = {
        "x": np.ascontiguousarray(np.asarray(x).T),
        "lora_down": np.ascontiguousarray(L0_tok_lora_down),
        "lora_up": np.ascontiguousarray(L0_tok_lora_up),
        "A_log": np.ascontiguousarray(L0_attn_A_log),
        "D": np.ascontiguousarray(np.asarray(L0_attn_D).reshape(1, DIM)),
        "xp_wT": np.ascontiguousarray(np.asarray(L0_attn_x_proj_w).T),
        "dt_wT": np.ascontiguousarray(np.asarray(L0_attn_dt_proj_w).T),
        "dt_b": np.ascontiguousarray(np.asarray(L0_attn_dt_proj_b).reshape(KT, P).T),
        "ffn_wT": np.ascontiguousarray(np.asarray(L0_ffn_weight).T),
        "ffn_b": np.ascontiguousarray(np.asarray(L0_ffn_bias).reshape(1, DIM)),
    }
    nc = bacc.Bacc("TRN2", target_bir_lowering=False, num_devices=1)
    d, feeds = {}, {}
    for name, a in arrays.items():
        feeds["in_" + name] = a
        d[name] = nc.dram_tensor("in_" + name, a.shape, mybir.dt.from_np(a.dtype), kind="ExternalInput").ap()
    out = nc.dram_tensor("out_h", (BATCH * SEQ, DIM), FP32, kind="ExternalOutput")
    d["out"] = out.ap()
    build(nc, d)
    r = run_bass_kernel_spmd(nc, [feeds], core_ids=[0])
    return r.results[0]["out_h"].reshape(BATCH, SEQ, DIM)
```
